# Optimizing a Trainium2 kernel written in Bass

```python
import numpy as np
import jax
import jax.numpy as jnp

def _softmax(x, axis=-1):
    return jax.nn.softmax(x, axis=axis)

def _gelu(x):
    return jax.nn.gelu(x, approximate=True)

def _silu(x):
    return jax.nn.silu(x)

def _sigmoid(x):
    return jax.nn.sigmoid(x)

def _layernorm(x, axis=-1, eps=1e-05):
    m = jnp.mean(x, axis=axis, keepdims=True)
    v = jnp.var(x, axis=axis, keepdims=True)
    return (x - m) / jnp.sqrt(v + eps)

def _scatter_add(tgt, idx, src, axis=0):
    return tgt.at[idx].add(src)

def _segment_sum(src, seg, n):
    return jax.ops.segment_sum(src, seg, n)
kernel_name = 'mk_cond_resid_d2_seqx_r8_5a7c06'

def setup_inputs(seed: int=0):
    np.random.seed(seed)
    _w = jnp.asarray

    def _rec_inputs():
        import jax
        import jax.numpy as jnp
        _rk = jax.random.key(seed)
        x = -0.0002071 + 1 * jax.random.normal(jax.random.fold_in(_rk, 1), (16, 128, 128), jnp.float32)
        _lenS = 128 - jax.random.randint(jax.random.fold_in(_rk, 7), (16,), 0, max(1, 128 // 4) + 1, jnp.int32)
        _lenS2 = 128 - jax.random.randint(jax.random.fold_in(_rk, 8), (16,), 0, max(1, 128 // 4) + 1, jnp.int32)
        cond_8 = jax.random.uniform(jax.random.fold_in(_rk, 11), (16, 8), jnp.float32, 0.0, 0.983423)
        return (x, cond_8)
    x, cond_8 = _rec_inputs()

    def _L0_cond_setup():
        import jax, jax.numpy as jnp
        import numpy as np
        R = 16
        ALPHA = 32.0
        SCALING = ALPHA / R
        key = jax.random.key(seed)
        ks = jax.random.split(key, 6)
        B, T, C, O, E = (16, 1500, 128, 128, 8)
        x = jax.random.normal(ks[0], (B, T, C), dtype=jnp.float32)
        w = jax.random.uniform(ks[1], (B, E), dtype=jnp.float32)
        W_base = jax.random.normal(ks[2], (O, C), dtype=jnp.float32) * 0.02
        b_base = jax.random.normal(ks[3], (O,), dtype=jnp.float32) * 0.02
        As = jax.random.normal(ks[4], (E, R, C), dtype=jnp.float32) * 0.02
        Bs = jax.random.normal(ks[5], (E, O, R), dtype=jnp.float32) * 0.02
        return {'x': x, 'w': w, 'W_base': W_base, 'b_base': b_base, 'As': As, 'Bs': Bs}
    _L0_cond_all = _L0_cond_setup()
    _L0_cond_in = {k: v for k, v in _L0_cond_all.items() if k in ('W_base', 'b_base', 'As', 'Bs')}
    del _L0_cond_all

    def _L1_cond_setup():
        import jax, jax.numpy as jnp
        import numpy as np
        TOP_K = 2
        NUM_MOE_LAYERS = 12

        def _gemma_mlp(x, gate_w, up_w, down_w):
            g = jnp.einsum('bsh,hi->bsi', x, gate_w)
            u = jnp.einsum('bsh,hi->bsi', x, up_w)
            return jnp.einsum('bsi,ih->bsh', jax.nn.gelu(g, approximate=True) * u, down_w)
        key = jax.random.key(seed)
        ks = jax.random.split(key, 8)
        B, S, H, I, E = (32, 32, 128, 512, 8)
        std = 0.02
        return {'x': jax.random.normal(ks[0], (B, S, H), jnp.float32), 'router_logits': jax.random.normal(ks[1], (B, E), jnp.float32), 'skill_gate': jax.random.normal(ks[2], (E, H, I), jnp.float32) * std, 'skill_up': jax.random.normal(ks[3], (E, H, I), jnp.float32) * std, 'skill_down': jax.random.normal(ks[4], (E, I, H), jnp.float32) * std, 'shared_gate': jax.random.normal(ks[5], (H, I), jnp.float32) * std, 'shared_up': jax.random.normal(ks[6], (H, I), jnp.float32) * std, 'shared_down': jax.random.normal(ks[7], (I, H), jnp.float32) * std}
    _L1_cond_all = _L1_cond_setup()
    _L1_cond_in = {k: v for k, v in _L1_cond_all.items() if k in ('skill_gate', 'skill_up', 'skill_down', 'shared_gate', 'shared_up', 'shared_down')}
    del _L1_cond_all
    return {'x': x, 'cond_8': cond_8, 'L0_cond_W_base': _L0_cond_in['W_base'], 'L0_cond_b_base': _L0_cond_in['b_base'], 'L0_cond_As': _L0_cond_in['As'], 'L0_cond_Bs': _L0_cond_in['Bs'], 'L1_cond_skill_gate': _L1_cond_in['skill_gate'], 'L1_cond_skill_up': _L1_cond_in['skill_up'], 'L1_cond_skill_down': _L1_cond_in['skill_down'], 'L1_cond_shared_gate': _L1_cond_in['shared_gate'], 'L1_cond_shared_up': _L1_cond_in['shared_up'], 'L1_cond_shared_down': _L1_cond_in['shared_down']}

def reference(x, cond_8, L0_cond_W_base, L0_cond_b_base, L0_cond_As, L0_cond_Bs, L1_cond_skill_gate, L1_cond_skill_up, L1_cond_skill_down, L1_cond_shared_gate, L1_cond_shared_up, L1_cond_shared_down):
    import jax
    import jax.numpy as jnp

    def _L0_cond_ref(x, w, W_base, b_base, As, Bs):
        import jax, jax.numpy as jnp
        import numpy as np
        R = 16
        ALPHA = 32.0
        SCALING = ALPHA / R
        out = jnp.einsum('btc,oc->bto', x, W_base) + b_base
        h = jnp.einsum('btc,erc->bter', x, As)
        lora = jnp.einsum('bter,eor,be->bto', h, Bs, w)
        return out + lora * SCALING

    def _L1_cond_ref(x, router_logits, skill_gate, skill_up, skill_down, shared_gate, shared_up, shared_down):
        import jax, jax.numpy as jnp
        import numpy as np
        TOP_K = 2
        NUM_MOE_LAYERS = 12

        def _gemma_mlp(x, gate_w, up_w, down_w):
            g = jnp.einsum('bsh,hi->bsi', x, gate_w)
            u = jnp.einsum('bsh,hi->bsi', x, up_w)
            return jnp.einsum('bsi,ih->bsh', jax.nn.gelu(g, approximate=True) * u, down_w)
        B = x.shape[0]
        E = skill_gate.shape[0]
        rw = jax.nn.softmax(router_logits.astype(jnp.float32), axis=-1)
        w, sel = jax.lax.top_k(rw, TOP_K)
        w = w / w.sum(axis=-1, keepdims=True)
        w = w.astype(x.dtype)
        scale = 1.0 / NUM_MOE_LAYERS
        w = scale * w + (1.0 - scale) * jax.lax.stop_gradient(w)
        dense_w = jnp.zeros((B, E), x.dtype).at[jnp.arange(B)[:, None], sel].add(w)

        def step(acc, params):
            g, u, d, we = params
            return (acc + we[:, None, None] * _gemma_mlp(x, g, u, d), None)
        out, _ = jax.lax.scan(step, jnp.zeros_like(x), (skill_gate, skill_up, skill_down, dense_w.T))
        out = out + _gemma_mlp(x, shared_gate, shared_up, shared_down)
        return out
    x = x + _L0_cond_ref(x, cond_8, L0_cond_W_base, L0_cond_b_base, L0_cond_As, L0_cond_Bs)
    x = x + _L1_cond_ref(x, cond_8, L1_cond_skill_gate, L1_cond_skill_up, L1_cond_skill_down, L1_cond_shared_gate, L1_cond_shared_up, L1_cond_shared_down)
    return x

_drawn_inputs = setup_inputs


def setup_inputs(seed=0):
    import zlib

    import numpy as np

    out = dict(_drawn_inputs(seed))
    spreads = {}
    factors = {'L0_cond_b_base': 2.833,
     'L1_cond_skill_gate': 6.454,
     'L1_cond_skill_up': 6.373,
     'L1_cond_skill_down': 6.376,
     'L1_cond_shared_gate': 4.61,
     'L1_cond_shared_up': 4.525,
     'L1_cond_shared_down': 4.518}
    for name, (base, spread) in spreads.items():
        noise = np.random.default_rng([zlib.crc32(name.encode()), seed]).standard_normal(out[name].shape)
        drawn = base * np.exp(spread * noise) if base else spread * noise
        out[name] = jnp.asarray(drawn.astype(out[name].dtype))
    for name, factor in factors.items():
        out[name] = (out[name] * factor).astype(out[name].dtype)
    return out
```

```python
from contextlib import ExitStack

import concourse.bass as bass
from concourse import mybir

F32 = mybir.dt.float32
F32R = mybir.dt.float32r
U32 = mybir.dt.uint32
I32 = mybir.dt.int32
ALU = mybir.AluOpType
ACT = mybir.ActivationFunctionType

LORA_SCALING = 2.0
GRAD_SCALE = 1.0 / 12.0


def lora_then_top2_moe(nc, x, cond, W_base, b_base, As, Bs, ex_gate, ex_up, ex_down,
                       sh_gate, sh_up, sh_down, out):
    B, S, H = x.shape
    E, _, I = ex_gate.shape
    R = As.shape[1]
    P = 128
    assert S == P and H == P and E * R == P and I == 512
    GB = I // S
    NG = B // GB
    NC = I // P
    SLOTS = 4
    RAW = 3 * I
    SPLIT = 2 * RAW
    G_HI, G_LO, U_HI, U_LO, DOWN = 0, I, 2 * I, 3 * I, 4 * I

    with ExitStack() as ctx:
        def sb(name, shape, dt=F32):
            return ctx.enter_context(nc.sbuf_tensor(name, shape, dt))

        def sem(name):
            return ctx.enter_context(nc.semaphore(name))

        cond_sb = sb("cond_sb", [B, E])
        a_sb = sb("a_sb", [P, H])
        b_nat = sb("b_nat", [H, E, R])
        w_nat = sb("w_nat", [H, H])
        bias = sb("bias", [H, 1])
        ident = sb("ident", [P, P])
        ones = sb("ones", [B, P])
        bT = sb("bT", [P, H])
        wT = sb("wT", [H, H])
        cond_er = sb("cond_er", [B, E, R])
        lora_s = sb("lora_s", [P, B])
        top8 = sb("top8", [B, 8])
        top_idx = sb("top_idx", [B, 8], U32)
        top_idxf = sb("top_idxf", [B, 2])
        rt = sb("rt", [B, 32])
        rdiag = sb("rdiag", [B, 4, B])
        wgt = sb("wgt", [P, 2, B])
        eidx = sb("eidx", [1, 2 * B], I32)

        xn = sb("xn", [P, B, H])
        xT = sb("xT", [P, B, S])
        sB = sb("sB", [P, 2, GB, H])
        work = sb("work", [P, 4, I])
        x1s = sb("x1s", [P, B, 2, S], F32R)
        s1T = sb("s1T", [P, I])
        raw_sh = sb("raw_sh", [P, RAW])
        raw_ex = sb("raw_ex", [P, SLOTS, RAW])
        wsh = sb("wsh", [P, SPLIT], F32R)
        wex = sb("wex", [P, E * SPLIT], F32R)
        hT_hi = sb("hT_hi", [P, 2, I], F32R)
        hT_lo = sb("hT_lo", [P, 2, I], F32R)
        xst = sb("xst", [P, 2, 2, S], F32R)

        def f32(ap):
            return ap.bitcast(F32)

        bank = [ctx.enter_context(nc.psum_tensor(f"bank{i}", [P, I], F32)) for i in range(8)]
        gate_ps = [bank[0], bank[2]]
        up_ps = [bank[1], bank[3]]

        ld_small = [sem(f"ld_{n}") for n in ("cond", "a", "b", "w", "bias")]
        ld_cond, ld_a, ld_b, ld_w, ld_bias = ld_small
        ld_x = [sem(f"ld_x{g}") for g in range(NG)]
        ld_sh = sem("ld_sh")
        ld_ex = [sem("ld_ex_even"), sem("ld_ex_odd")]
        consts = sem("consts")
        ident_zero = sem("ident_zero")
        rt_step = sem("rt_step")
        exp_done = sem("exp_done")
        cond_er_ready = sem("cond_er_ready")
        setup_ps = sem("setup_ps")
        setup_sb = sem("setup_sb")
        sB_ready = sem("sB_ready")
        xT_ps = sem("xT_ps")
        xT_ready = sem("xT_ready")
        delta_ps = sem("delta_ps")
        weff_ready = sem("weff_ready")
        x1_ps = sem("x1_ps")
        x1_ready = sem("x1_ready")
        x1hi_ready = sem("x1hi_ready")
        x1lo_ready = sem("x1lo_ready")
        sh_hi = sem("sh_hi")
        sh_lo = sem("sh_lo")
        sh_dhi = sem("sh_dhi")
        sh_dlo = sem("sh_dlo")
        ex_hi = sem("ex_hi")
        ex_lo = sem("ex_lo")
        ex_dhi = sem("ex_dhi")
        ex_dlo = sem("ex_dlo")
        gate_done = sem("gate_done")
        up_done = sem("up_done")
        gelu_done = sem("gelu_done")
        h_done = sem("h_done")
        hT_done = sem("hT_done")
        hi_done = sem("hi_done")
        lo_done = sem("lo_done")
        down_done = sem("down_done")
        sum_done = sem("sum_done")
        sumT_done = sem("sumT_done")
        base_done = sem("base_done")
        xst_ready = sem("xst_ready")
        acc_done = sem("acc_done")
        out_ready = sem("out_ready")
        st_out = sem("st_out")

        gelu_sb = [work[:, 0, :], work[:, 1, :]]
        h_sb = [work[:, 2, :], work[:, 3, :]]
        base = xT

        def x1_hi(g):
            return x1s[:, bass.ds(g * GB, GB), 0, :]

        def x1_lo(g):
            return x1s[:, bass.ds(g * GB, GB), 1, :]

        NU = NG * NC
        NE = 2 * B

        block = ctx.enter_context(nc.Block())

        @block.sync
        def _(sp):
            sp.dma_start(cond_sb[:, :], cond).then_inc(ld_cond, 16)
            sp.dma_start(xn[:, 0:GB, :], x[0:GB].rearrange("b s h -> s b h")).then_inc(ld_x[0], 16)
            sp.dma_start(w_nat[:, :], W_base).then_inc(ld_w, 16)
            for g in range(1, NG):
                sp.dma_start(xn[:, g * GB:(g + 1) * GB, :],
                             x[g * GB:(g + 1) * GB].rearrange("b s h -> s b h")).then_inc(ld_x[g], 16)
            sp.dma_start(raw_sh[:, 0:I], sh_gate).then_inc(ld_sh, 16)
            sp.dma_start(raw_sh[:, I:2 * I], sh_up).then_inc(ld_sh, 16)
            sp.dma_start(raw_sh[:, 2 * I:RAW].rearrange("p (c h) -> p c h", c=NC),
                         sh_down.rearrange("(c p) h -> p c h", p=P)).then_inc(ld_sh, 16)
            for e in range(E):
                if e >= 2:
                    sp.wait_ge(ld_ex[e % 2], 48 * (e // 2))
                if e >= SLOTS:
                    sp.wait_ge(ex_lo, 2 * (e - SLOTS) + 2)
                    sp.wait_ge(ex_dlo, e - SLOTS + 1)
                slot = raw_ex[:, e % SLOTS, :]
                sp.dma_start(slot[:, 0:I], ex_gate[e]).then_inc(ld_ex[e % 2], 16)
                sp.dma_start(slot[:, I:2 * I], ex_up[e]).then_inc(ld_ex[e % 2], 16)
                sp.dma_start(slot[:, 2 * I:RAW].rearrange("p (c h) -> p c h", c=NC),
                             ex_down[e].rearrange("(c p) h -> p c h", p=P)).then_inc(ld_ex[e % 2], 16)
            with sp.Fori(0, B) as b:
                sp.wait_ge(out_ready, b + 1)
                sp.dma_start(out[bass.ds(b, 1)].rearrange("b s h -> s (b h)"),
                             base[:, bass.ds(b, 1), :].rearrange("p b h -> p (b h)")).then_inc(st_out, 16)
            sp.wait_ge(st_out, 16 * B)

        @block.gpsimd
        def _(pool):
            pool.memset(ident[:, :], 0.0).then_inc(ident_zero, 1)
            pool.memset(ones[:, :], 1.0).then_inc(consts, 1)
            pool.wait_ge(ident_zero, 1)
            pool.affine_select(out=ident[:, :], in_=ident[:, :], compare_op=ALU.not_equal, fill=1.0,
                               base=0, pattern=[[-1, P]], channel_multiplier=1).then_inc(consts, 1)

            pool.wait_ge(setup_sb, 2)
            for g in range(NG):
                if g >= 2:
                    pool.wait_ge(delta_ps, g - 1)
                for j in range(GB):
                    b = g * GB + j
                    pool.tensor_scalar(sB[:, g % 2, j, :], bT[:, :], lora_s[:, b:b + 1], None,
                                       ALU.mult).then_inc(sB_ready, 1)

            def split_down(raw, dst, hi_sem, lo_sem, n):
                src = raw[:, 2 * I:RAW].rearrange("p (c h) -> p c h", c=NC)
                d = dst.rearrange("p (c v h) -> p c v h", c=NC, v=2)
                pool.tensor_copy(d[:, :, 0, :], src).then_inc(hi_sem, 1)
                pool.wait_ge(hi_sem, n)
                pool.tensor_tensor(d[:, :, 1, :], src, f32(d[:, :, 0, :]), ALU.subtract).then_inc(lo_sem, 1)

            pool.wait_ge(ld_sh, 48)
            split_down(raw_sh[:, :], wsh[:, DOWN:SPLIT], sh_dhi, sh_dlo, 1)
            for e in range(E):
                pool.wait_ge(ld_ex[e % 2], 48 * (e // 2 + 1))
                split_down(raw_ex[:, e % SLOTS, :], wex[:, e * SPLIT + DOWN:(e + 1) * SPLIT],
                           ex_dhi, ex_dlo, e + 1)

            def stage(b, j):
                pool.tensor_copy(xst[:, j, :, :], f32(x1s[:, bass.ds(b, 1), :, :]).rearrange("p a v s -> p (a v) s")
                                 ).then_inc(xst_ready, 1)

            pool.wait_ge(x1lo_ready, NG)
            for j in range(2):
                stage(j, j)
            with pool.Fori(1, B // 2) as i:
                for j in range(2):
                    pool.wait_ge(up_done, 4 * i + (NU + 2 * j - 2))
                    stage(2 * i + j, j)

        @block.scalar
        def _(act):
            act.dma_start(b_nat[:, :, :], Bs.rearrange("e o r -> o e r")).then_inc(ld_b, 16)
            act.dma_start(a_sb[:, :], As.rearrange("e r c -> (e r) c")).then_inc(ld_a, 16)
            act.dma_start(bias[:, :], b_base.rearrange("(o a) -> o a", a=1)).then_inc(ld_bias, 16)
            act.wait_ge(rt_step, 3)
            act.activation(rt[:, 8:16], top8[:, :], ACT.Exp, bias=rt[:, 0:1],
                           accum_out=rt[:, 1:2]).then_inc(exp_done, 1)
            for g in range(NG):
                act.wait_ge(xT_ps, g + 1)
                act.copy(xT[:, g * GB:(g + 1) * GB, :], bank[g][:, :].rearrange("p (b s) -> p b s", b=GB)
                         ).then_inc(xT_ready, 1)
            for g in range(NG):
                if g < 2:
                    act.wait_ge(ld_sh, 48)
                    act.copy(wsh[:, 2 * g * I:(2 * g + 1) * I], raw_sh[:, g * I:(g + 1) * I]).then_inc(sh_hi, 1)
                act.wait_ge(x1_ready, g + 1)
                act.copy(x1_hi(g), xn[:, g * GB:(g + 1) * GB, :]).then_inc(x1hi_ready, 1)

            def gelu(t, q):
                act.wait_ge(gate_done, t + 1)
                if not (isinstance(t, int) and t < 2):
                    act.wait_ge(h_done, t - 1)
                act.activation(gelu_sb[q], gate_ps[q][:, :], ACT.Gelu_apprx_tanh).then_inc(gelu_done, 1)

            def hi_shared(t, q):
                act.wait_ge(h_done, t + 1)
                if not (isinstance(t, int) and t < 2):
                    act.wait_ge(down_done, t - 1)
                act.copy(hT_hi[:, q, :], h_sb[q]).then_inc(hi_done, 1)

            def hi_expert(t, q):
                act.wait_ge(hT_done, t - (NU - 1))
                act.wait_ge(down_done, t - 1)
                act.copy(hT_hi[:, q, :], bank[6 + q][:, :]).then_inc(hi_done, 1)

            def split_hi(g, c):
                half = c % 2
                e = 2 * g + c // 2
                act.wait_ge(ld_ex[c // 2], 48 * g + 48)
                act.copy(wex[:, bass.ds(e * SPLIT + 2 * half * I, I)],
                         raw_ex[:, bass.ds(e % SLOTS, 1), half * I:(half + 1) * I].rearrange("p a n -> p (a n)")
                         ).then_inc(ex_hi, 1)

            def base_copy(g):
                act.wait_ge(sumT_done, g + 1)
                act.copy(base[:, bass.ds(g * GB, GB), :],
                         bank[5][:, :].rearrange("p (b s) -> p b s", b=GB)).then_inc(base_done, 1)

            def shared_group(g):
                for c in range(NC):
                    t = NC * g + c
                    gelu(t, c % 2)
                    if not (isinstance(t, int) and t == 0):
                        hi_shared(t - 1, (c + 1) % 2)
                    split_hi(g, c)
                    if c == 3 and not (isinstance(g, int) and g == 0):
                        base_copy(g - 1)

            shared_group(0)
            with act.Fori(1, NG) as g:
                shared_group(g)
            for n in range(4):
                gelu(NU + n, n % 2)
                if n == 0:
                    hi_shared(NU - 1, 1)
                else:
                    hi_expert(NU + n - 1, (n + 1) % 2)
                if n == 3:
                    base_copy(NG - 1)
            with act.Fori(1, B // 2) as i:
                for n in range(4):
                    gelu(4 * i + (NU + n), n % 2)
                    hi_expert(4 * i + (NU + n - 1), (n + 1) % 2)
            hi_expert(NU + NE - 1, 1)

        @block.vector
        def _(dve):
            dve.wait_ge(ld_cond, 16)
            dve.tensor_scalar(cond_er[:, :, :], cond_sb[:, :].rearrange("b (e a) -> b e a", a=1).to_broadcast([B, E, R]),
                              LORA_SCALING, None, ALU.mult).then_inc(cond_er_ready, 1)
            dve.max(top8[:, :], cond_sb[:, :]).then_inc(rt_step, 1)
            dve.wait_ge(rt_step, 1)
            dve.max_index(top_idx[:, :], top8[:, :], cond_sb[:, :]).then_inc(rt_step, 1)
            dve.tensor_scalar(rt[:, 0:1], top8[:, 0:1], -1.0, None, ALU.mult).then_inc(rt_step, 1)
            dve.wait_ge(exp_done, 1)
            dve.reciprocal(rt[:, 2:3], rt[:, 1:2]).then_inc(rt_step, 1)
            dve.wait_ge(rt_step, 4)
            dve.tensor_scalar(rt[:, 16:18], rt[:, 8:10], rt[:, 2:3], None, ALU.mult).then_inc(rt_step, 1)
            dve.wait_ge(rt_step, 5)
            dve.tensor_tensor(rt[:, 3:4], rt[:, 16:17], rt[:, 17:18], ALU.add).then_inc(rt_step, 1)
            dve.wait_ge(rt_step, 6)
            dve.reciprocal(rt[:, 4:5], rt[:, 3:4]).then_inc(rt_step, 1)
            dve.wait_ge(rt_step, 7)
            dve.tensor_scalar(rt[:, 18:20], rt[:, 16:18], rt[:, 4:5], None, ALU.mult).then_inc(rt_step, 1)
            dve.wait_ge(rt_step, 8)
            dve.tensor_scalar(rt[:, 20:22], rt[:, 18:20], GRAD_SCALE, None, ALU.mult).then_inc(rt_step, 1)
            dve.wait_ge(rt_step, 9)
            dve.scalar_tensor_tensor(rt[:, 22:24], rt[:, 18:20], 1.0 - GRAD_SCALE, rt[:, 20:22],
                                     ALU.mult, ALU.add).then_inc(rt_step, 1)
            dve.tensor_copy(top_idxf[:, :], top_idx[:, 0:2]).then_inc(rt_step, 1)
            dve.wait_ge(consts, 2)
            dve.wait_ge(rt_step, 11)
            for k in range(2):
                dve.tensor_scalar(rdiag[:, k, :], ident[0:B, 0:B], rt[:, 22 + k:23 + k], None,
                                  ALU.mult).then_inc(rt_step, 1)
            for k in range(2):
                dve.tensor_scalar(rdiag[:, 2 + k, :], ident[0:B, 0:B], top_idxf[:, k:k + 1], None,
                                  ALU.mult).then_inc(rt_step, 1)

            dve.wait_ge(setup_ps, 1)
            dve.tensor_copy(lora_s[:, :], bank[6][:, 0:B]).then_inc(setup_sb, 1)
            dve.wait_ge(setup_ps, 2)
            dve.tensor_copy(bT[:, :], bank[4][:, 0:H]).then_inc(setup_sb, 1)
            dve.wait_ge(setup_ps, 3)
            dve.tensor_copy(wT[:, :], bank[5][:, 0:H]).then_inc(setup_sb, 1)
            dve.wait_ge(setup_sb, 3)
            for g in range(NG):
                dve.wait_ge(delta_ps, g + 1)
                dve.tensor_tensor(work[:, g, :].rearrange("p (b o) -> p b o", b=GB),
                                  bank[4 + g][:, :].rearrange("p (b o) -> p b o", b=GB),
                                  wT[:, :].rearrange("p (a o) -> p a o", a=1).to_broadcast([P, GB, H]),
                                  ALU.add).then_inc(weff_ready, 1)
            dve.wait_ge(ld_bias, 16)
            for g in range(NG):
                dve.wait_ge(x1_ps, g + 1)
                dve.wait_ge(xT_ready, g + 1)
                dve.scalar_tensor_tensor(xn[:, g * GB:(g + 1) * GB, :],
                                         bank[g][:, :].rearrange("p (b s) -> p b s", b=GB), bias[:, 0:1],
                                         xT[:, g * GB:(g + 1) * GB, :], ALU.add, ALU.add).then_inc(x1_ready, 1)
                if g < 2:
                    dve.wait_ge(sh_hi, g + 1)
                    dve.tensor_tensor(wsh[:, (2 * g + 1) * I:(2 * g + 2) * I], raw_sh[:, g * I:(g + 1) * I],
                                      f32(wsh[:, 2 * g * I:(2 * g + 1) * I]), ALU.subtract).then_inc(sh_lo, 1)
                dve.wait_ge(x1hi_ready, g + 1)
                dve.tensor_tensor(x1_lo(g), xn[:, g * GB:(g + 1) * GB, :], f32(x1_hi(g)),
                                  ALU.subtract).then_inc(x1lo_ready, 1)
            dve.wait_ge(setup_ps, 4)
            dve.tensor_copy(wgt[:, :, :], bank[7][:, 0:2 * B].rearrange("p (k b) -> p k b", k=2)
                            ).then_inc(setup_sb, 1)
            dve.tensor_copy(eidx[:, :].rearrange("p (b k) -> p k b", k=2),
                            bank[7][0:1, 2 * B:4 * B].rearrange("p (k b) -> p k b", k=2)).then_inc(setup_sb, 1)

            def h_shared(t, q):
                dve.wait_ge(up_done, t + 1)
                dve.wait_ge(gelu_done, t + 1)
                if not (isinstance(t, int) and t < 2):
                    dve.wait_ge(lo_done, t - 1)
                dve.tensor_tensor(h_sb[q], up_ps[q][:, :], gelu_sb[q], ALU.mult).then_inc(h_done, 1)

            def h_expert(t, q, b, k):
                dve.wait_ge(up_done, t + 1)
                dve.wait_ge(gelu_done, t + 1)
                if isinstance(t, int) and t < NU + 2:
                    dve.wait_ge(lo_done, t - 1)
                dve.scalar_tensor_tensor(h_sb[q], up_ps[q][:, :], wgt[:, k, bass.ds(b, 1)], gelu_sb[q],
                                         ALU.mult, ALU.mult).then_inc(h_done, 1)

            def lo(t, q, src):
                dve.wait_ge(hi_done, t + 1)
                if not (isinstance(t, int) and t < 2):
                    dve.wait_ge(down_done, t - 1)
                dve.tensor_tensor(hT_lo[:, q, :], src, f32(hT_hi[:, q, :]), ALU.subtract).then_inc(lo_done, 1)

            def split_lo(g, c):
                half = c % 2
                e = 2 * g + c // 2
                dve.wait_ge(ex_hi, NC * g + (c + 1))
                dve.tensor_tensor(wex[:, bass.ds(e * SPLIT + (2 * half + 1) * I, I)],
                                  raw_ex[:, bass.ds(e % SLOTS, 1), half * I:(half + 1) * I].rearrange("p a n -> p (a n)"),
                                  f32(wex[:, bass.ds(e * SPLIT + 2 * half * I, I)]),
                                  ALU.subtract).then_inc(ex_lo, 1)

            def sum_group(g):
                dve.wait_ge(down_done, NC * g + NC)
                if not (isinstance(g, int) and g == 0):
                    dve.wait_ge(sumT_done, g)
                dve.tensor_tensor(s1T[:, :].rearrange("p (b s) -> p b s", b=GB),
                                  bank[4][:, :].rearrange("p (b s) -> p b s", b=GB),
                                  xn[:, bass.ds(g * GB, GB), :], ALU.add).then_inc(sum_done, 1)

            def shared_group(g):
                for c in range(NC):
                    t = NC * g + c
                    h_shared(t, c % 2)
                    if not (isinstance(t, int) and t == 0):
                        lo(t - 1, (c + 1) % 2, h_sb[(c + 1) % 2])
                    if c == 1 and not (isinstance(g, int) and g == 0):
                        sum_group(g - 1)
                    split_lo(g, c)

            def result(b, j):
                of_b = base[:, bass.ds(b, 1), :].rearrange("p a h -> p (a h)")
                dve.wait_ge(down_done, 2 * b + (NU + 2))
                dve.tensor_tensor(of_b, bank[4 + j][:, 0:H], of_b, ALU.add).then_inc(acc_done, 1)
                dve.wait_ge(acc_done, b + 1)
                dve.tensor_tensor(of_b, bank[4 + j][:, H:2 * H], of_b, ALU.add).then_inc(out_ready, 1)

            shared_group(0)
            with dve.Fori(1, NG) as g:
                shared_group(g)
            dve.wait_ge(setup_sb, 5)
            for n in range(4):
                h_expert(NU + n, n % 2, n // 2, n % 2)
                if n == 0:
                    lo(NU - 1, 1, h_sb[1])
                else:
                    lo(NU + n - 1, (n + 1) % 2, bank[6 + (n + 1) % 2][:, :])
                if n == 1:
                    sum_group(NG - 1)
                if n == 3:
                    dve.wait_ge(base_done, NG)
                    result(0, 0)
            with dve.Fori(1, B // 2) as i:
                for n in range(4):
                    h_expert(4 * i + (NU + n), n % 2, 2 * i + n // 2, n % 2)
                    lo(4 * i + (NU + n - 1), (n + 1) % 2, bank[6 + (n + 1) % 2][:, :])
                    if n == 1:
                        result(2 * i - 1, 1)
                    if n == 3:
                        result(2 * i, 0)
            lo(NU + NE - 1, 1, bank[7][:, :])
            result(B - 1, 1)

        @block.tensor
        def _(pe):
            pe.wait_ge(consts, 2)
            pe.wait_ge(cond_er_ready, 1)
            pe.transpose(bank[6][:, 0:B], cond_er[:, :, :].rearrange("b e r -> b (e r)"), ident[0:B, 0:B]
                         ).then_inc(setup_ps, 1)
            pe.wait_ge(ld_b, 16)
            pe.transpose(bank[4][:, 0:H], b_nat[:, :, :].rearrange("o e r -> o (e r)"), ident[:, :]
                         ).then_inc(setup_ps, 1)
            pe.wait_ge(ld_w, 16)
            pe.transpose(bank[5][:, 0:H], w_nat[:, :], ident[:, :]).then_inc(setup_ps, 1)
            for g in range(NG):
                pe.wait_ge(ld_x[g], 16)
                for j in range(GB):
                    mm = pe.transpose(bank[g][:, j * S:(j + 1) * S], xn[:, g * GB + j, :], ident[:, :])
                mm.then_inc(xT_ps, 1)
            pe.wait_ge(ld_a, 16)
            pe.wait_ge(setup_sb, 3)
            for g in range(NG):
                pe.wait_ge(sB_ready, GB * (g + 1))
                pe.matmul(bank[4 + g][:, :], a_sb[:, :], sB[:, g % 2, :, :].rearrange("p b o -> p (b o)"),
                          start=True, stop=True).then_inc(delta_ps, 1)
            for g in range(NG):
                pe.wait_ge(weff_ready, g + 1)
                pe.wait_ge(xT_ready, g + 1)
                for j in range(GB):
                    mm = pe.matmul(bank[g][:, j * S:(j + 1) * S], work[:, g, j * H:(j + 1) * H],
                                   xT[:, g * GB + j, :], start=True, stop=True)
                mm.then_inc(x1_ps, 1)
            pe.wait_ge(rt_step, 15)
            pe.matmul(bank[7][:, 0:4 * B], ones[:, :], rdiag[:, :, :].rearrange("p k b -> p (k b)"),
                      start=True, stop=True).then_inc(setup_ps, 1)

            def gate_up_shared(g, c):
                q = c % 2
                t = NC * g + c
                if isinstance(t, int) and t < 2:
                    pe.wait_ge(x1_ready, 2 * t + 2)
                else:
                    pe.wait_ge(h_done, t - 1)
                if c == 0:
                    pe.wait_ge(x1lo_ready, g + 1)
                for first, ps, done in ((G_HI, gate_ps[q], gate_done), (U_HI, up_ps[q], up_done)):
                    w_hi = wsh[:, first + c * P:first + (c + 1) * P]
                    w_lo = wsh[:, first + I + c * P:first + I + (c + 1) * P]
                    pe.matmul(ps[:, :], w_hi, x1_hi(g), start=True, stop=False)
                    pe.matmul(ps[:, :], w_hi, x1_lo(g), start=False, stop=False)
                    pe.matmul(ps[:, :], w_lo, x1_hi(g), start=False, stop=True).then_inc(done, 1)

            def down_shared(g, c):
                q = c % 2
                pe.wait_ge(lo_done, NC * g + (c + 1))
                if c == 0 and not (isinstance(g, int) and g == 0):
                    pe.wait_ge(sum_done, g)
                w_hi = wsh[:, DOWN + 2 * c * H:DOWN + (2 * c + 1) * H]
                w_lo = wsh[:, DOWN + (2 * c + 1) * H:DOWN + (2 * c + 2) * H]
                pe.matmul(bank[4][:, :], w_hi, hT_hi[:, q, :], start=(c == 0), stop=False)
                pe.matmul(bank[4][:, :], w_hi, hT_lo[:, q, :], start=False, stop=False)
                pe.matmul(bank[4][:, :], w_lo, hT_hi[:, q, :], start=False, stop=(c == NC - 1)
                          ).then_inc(down_done, 1)

            def sum_transposes(g):
                pe.wait_ge(sum_done, g + 1)
                if not (isinstance(g, int) and g == 0):
                    pe.wait_ge(base_done, g)
                for j in range(GB):
                    mm = pe.transpose(bank[5][:, j * H:(j + 1) * H], s1T[:, j * S:(j + 1) * S], ident[:, :])
                mm.then_inc(sumT_done, 1)

            def shared_group(g):
                first = isinstance(g, int) and g == 0
                for c in range(NC):
                    gate_up_shared(g, c)
                    if c >= 2:
                        down_shared(g, c - 2)
                    elif not first:
                        down_shared(g - 1, c + 2)
                    if c == 2 and not first:
                        sum_transposes(g - 1)

            def gate_up_expert(n, q, j, batches):
                w0 = pe.value_load(eidx[0:1, bass.ds(n, 1)], min_val=0, max_val=E - 1) * SPLIT
                pe.wait_ge(h_done, n + (NU - 1))
                if q == 0:
                    pe.wait_ge(xst_ready, batches)
                for first, ps, done in ((G_HI, gate_ps[q], gate_done), (U_HI, up_ps[q], up_done)):
                    pe.matmul(ps[:, :], xst[:, j, 0, :], wex[:, bass.ds(w0 + first, I)], start=True, stop=False)
                    pe.matmul(ps[:, :], xst[:, j, 0, :], wex[:, bass.ds(w0 + (first + I), I)], start=False, stop=False)
                    pe.matmul(ps[:, :], xst[:, j, 1, :], wex[:, bass.ds(w0 + first, I)], start=False, stop=True
                              ).then_inc(done, 1)

            def h_transposes(n, q):
                pe.wait_ge(h_done, n + (NU + 1))
                if not (isinstance(n, int) and n < 2):
                    pe.wait_ge(lo_done, n + (NU - 1))
                for c in range(NC):
                    mm = pe.transpose(bank[6 + q][:, c * P:(c + 1) * P], h_sb[q][:, c * P:(c + 1) * P], ident[:, :])
                mm.then_inc(hT_done, 1)

            def down_expert(n, q, k, j):
                y = bank[4 + j]
                w0 = pe.value_load(eidx[0:1, bass.ds(n, 1)], min_val=0, max_val=E - 1) * SPLIT
                pe.wait_ge(lo_done, n + (NU + 1))
                if k == 0 and j == 1:
                    pe.wait_ge(base_done, NG)
                for c in range(NC):
                    at = DOWN + 2 * c * H
                    hT = hT_hi[:, q, c * P:(c + 1) * P]
                    pe.matmul(y[:, 0:2 * H], hT, wex[:, bass.ds(w0 + at, 2 * H)],
                              start=(k == 0 and c == 0), stop=False, skip_group_check=True)
                    mm = pe.matmul(y[:, 0:H], hT_lo[:, q, c * P:(c + 1) * P], wex[:, bass.ds(w0 + at, H)],
                                   start=False, stop=(k == 1 and c == NC - 1), skip_group_check=True)
                mm.then_inc(down_done, 1)

            pe.wait_ge(sh_lo, 2)
            pe.wait_ge(sh_dlo, 1)
            shared_group(0)
            with pe.Fori(1, NG) as g:
                shared_group(g)
            down_shared(NG - 1, NC - 2)
            pe.wait_ge(ex_lo, 2 * E)
            pe.wait_ge(ex_dlo, E)
            pe.wait_ge(setup_sb, 5)
            for n in range(4):
                gate_up_expert(n, n % 2, n // 2, n // 2 + 1)
                if n >= 1:
                    h_transposes(n - 1, (n + 1) % 2)
                if n == 1:
                    down_shared(NG - 1, NC - 1)
                if n == 2:
                    sum_transposes(NG - 1)
                if n >= 2:
                    down_expert(n - 2, n % 2, n % 2, 0)
            with pe.Fori(1, B // 2) as i:
                for n in range(4):
                    gate_up_expert(4 * i + n, n % 2, n // 2, 2 * i + (n // 2 + 1))
                    h_transposes(4 * i + (n - 1), (n + 1) % 2)
                    down_expert(4 * i + (n - 2), n % 2, n % 2, (n // 2 + 1) % 2)
            h_transposes(NE - 1, 1)
            down_expert(NE - 2, 0, 0, 1)
            down_expert(NE - 1, 1, 1, 1)


_INS = ["x", "cond_8", "L0_cond_W_base", "L0_cond_b_base", "L0_cond_As", "L0_cond_Bs",
        "L1_cond_skill_gate", "L1_cond_skill_up", "L1_cond_skill_down",
        "L1_cond_shared_gate", "L1_cond_shared_up", "L1_cond_shared_down"]
_OUTS = [((16, 128, 128), "float32")]


def kernel(**inputs):
    import numpy as _np
    import concourse.bacc as _bacc
    from concourse import mybir as _mybir
    from concourse.bass_utils import run_bass_kernel_spmd as _run

    nc = _bacc.Bacc("TRN2", target_bir_lowering=False, num_devices=1)
    arrays, args = {}, []
    for name in _INS:
        a = _np.ascontiguousarray(inputs[name])
        arrays[f"in_{name}_dram"] = a
        args.append(nc.dram_tensor(f"in_{name}_dram", a.shape, _mybir.dt.from_np(a.dtype), kind="ExternalInput").ap())
    for i, (shape, dtype) in enumerate(_OUTS):
        dt = _mybir.dt.from_np(_np.dtype(dtype))
        args.append(nc.dram_tensor(f"out_{i}_dram", shape, dt, kind="ExternalOutput").ap())
    lora_then_top2_moe(nc, *args)
    r = _run(nc, [arrays], core_ids=[0])
    return r.results[0]["out_0_dram"]
```

```python
from contextlib import ExitStack

import concourse.bass as bass
from concourse import mybir

F32 = mybir.dt.float32
F32R = mybir.dt.float32r
U32 = mybir.dt.uint32
I32 = mybir.dt.int32
ALU = mybir.AluOpType
ACT = mybir.ActivationFunctionType

LORA_SCALING = 2.0
GRAD_SCALE = 1.0 / 12.0


def lora_then_top2_moe(nc, x, cond, W_base, b_base, As, Bs, ex_gate, ex_up, ex_down,
                       sh_gate, sh_up, sh_down, out):
    B, S, H = x.shape
    E, _, I = ex_gate.shape
    R = As.shape[1]
    P = 128
    assert S == P and H == P and E * R == P and I == 512
    GB = I // S
    NG = B // GB
    NC = I // P
    SLOTS = 4
    RAW = 3 * I
    SPLIT = 2 * RAW
    G_HI, G_LO, U_HI, U_LO, DOWN = 0, I, 2 * I, 3 * I, 4 * I

    with ExitStack() as ctx:
        def sb(name, shape, dt=F32):
            return ctx.enter_context(nc.sbuf_tensor(name, shape, dt))

        def sem(name):
            return ctx.enter_context(nc.semaphore(name))

        cond_sb = sb("cond_sb", [B, E])
        a_sb = sb("a_sb", [P, H])
        b_nat = sb("b_nat", [H, E, R])
        w_nat = sb("w_nat", [H, H])
        bias = sb("bias", [H, 1])
        ident = sb("ident", [P, P])
        ones = sb("ones", [B, P])
        bT = sb("bT", [P, H])
        wT = sb("wT", [H, H])
        cond_er = sb("cond_er", [B, E, R])
        lora_s = sb("lora_s", [P, B])
        top8 = sb("top8", [B, 8])
        top_idx = sb("top_idx", [B, 8], U32)
        top_idxf = sb("top_idxf", [B, 2])
        rt = sb("rt", [B, 32])
        rdiag = sb("rdiag", [B, 4, B])
        wgt = sb("wgt", [P, 2, B])
        eidx = sb("eidx", [1, 2 * B], I32)

        xn = sb("xn", [P, B, H])
        xT = sb("xT", [P, B, S])
        sB = sb("sB", [P, 2, GB, H])
        work = sb("work", [P, 4, I])
        x1s = sb("x1s", [P, B, 2, S], F32R)
        s1T = sb("s1T", [P, I])
        raw_sh = sb("raw_sh", [P, RAW])
        raw_ex = sb("raw_ex", [P, SLOTS, RAW])
        wsh = sb("wsh", [P, SPLIT], F32R)
        wex = sb("wex", [P, E * SPLIT], F32R)
        hT_hi = sb("hT_hi", [P, 2, I], F32R)
        hT_lo = sb("hT_lo", [P, 2, I], F32R)
        xst = sb("xst", [P, 2, 2, S], F32R)

        def f32(ap):
            return ap.bitcast(F32)

        bank = [ctx.enter_context(nc.psum_tensor(f"bank{i}", [P, I], F32)) for i in range(8)]
        gate_ps = [bank[0], bank[2]]
        up_ps = [bank[1], bank[3]]

        ld_small = [sem(f"ld_{n}") for n in ("cond", "a", "b", "w", "bias")]
        ld_cond, ld_a, ld_b, ld_w, ld_bias = ld_small
        ld_x = [sem(f"ld_x{g}") for g in range(NG)]
        ld_sh_gate = sem("ld_sh_gate")
        ld_sh_up = sem("ld_sh_up")
        ld_sh_down = sem("ld_sh_down")
        ld_ex = [sem("ld_ex_even"), sem("ld_ex_odd")]
        consts = sem("consts")
        ident_zero = sem("ident_zero")
        rt_step = sem("rt_step")
        exp_done = sem("exp_done")
        gelu_table = sem("gelu_table")
        cond_er_ready = sem("cond_er_ready")
        setup_ps = sem("setup_ps")
        setup_sb = sem("setup_sb")
        sB_ready = sem("sB_ready")
        xT_ps = sem("xT_ps")
        xT_ready = sem("xT_ready")
        delta_ps = sem("delta_ps")
        weff_ready = sem("weff_ready")
        x1_ps = sem("x1_ps")
        x1_ready = sem("x1_ready")
        x1hi_ready = sem("x1hi_ready")
        x1lo_ready = sem("x1lo_ready")
        sh_hi = sem("sh_hi")
        sh_lo = sem("sh_lo")
        sh_glo = sem("sh_glo")
        sh_dhi = sem("sh_dhi")
        sh_dlo = sem("sh_dlo")
        ex_hi = sem("ex_hi")
        ex_lo = sem("ex_lo")
        ex_dhi = sem("ex_dhi")
        ex_dlo = sem("ex_dlo")
        gate_done = sem("gate_done")
        up_done = sem("up_done")
        gelu_done = sem("gelu_done")
        h_done = sem("h_done")
        hT_done = sem("hT_done")
        hi_done = sem("hi_done")
        lo_done = sem("lo_done")
        down_done = sem("down_done")
        sum_done = sem("sum_done")
        sumT_done = sem("sumT_done")
        base_done = sem("base_done")
        xst_ready = sem("xst_ready")
        acc_done = sem("acc_done")
        out_ready = sem("out_ready")
        st_out = sem("st_out")

        gelu_sb = [work[:, 0, :], work[:, 1, :]]
        h_sb = [work[:, 2, :], work[:, 3, :]]
        base = xT

        def x1_hi(g):
            return x1s[:, bass.ds(g * GB, GB), 0, :]

        def x1_lo(g):
            return x1s[:, bass.ds(g * GB, GB), 1, :]

        NU = NG * NC
        NE = 2 * B

        block = ctx.enter_context(nc.Block())

        @block.sync
        def _(sp):
            sp.dma_start(cond_sb[:, :], cond).then_inc(ld_cond, 16)
            sp.dma_start(xn[:, 0:GB, :], x[0:GB].rearrange("b s h -> s b h")).then_inc(ld_x[0], 16)
            sp.dma_start(w_nat[:, :], W_base).then_inc(ld_w, 16)

            def load_x(g):
                sp.dma_start(xn[:, g * GB:(g + 1) * GB, :],
                             x[g * GB:(g + 1) * GB].rearrange("b s h -> s b h")).then_inc(ld_x[g], 16)

            load_x(1)
            sp.dma_start(raw_sh[:, 0:I], sh_gate).then_inc(ld_sh_gate, 16)
            load_x(2)
            sp.dma_start(raw_sh[:, I:2 * I], sh_up).then_inc(ld_sh_up, 16)
            load_x(3)
            sp.dma_start(raw_sh[:, 2 * I:RAW].rearrange("p (c h) -> p c h", c=NC),
                         sh_down.rearrange("(c p) h -> p c h", p=P)).then_inc(ld_sh_down, 16)
            for e in range(E):
                if e >= 2:
                    sp.wait_ge(ld_ex[e % 2], 48 * (e // 2))
                if e >= SLOTS:
                    sp.wait_ge(ex_lo, 2 * (e - SLOTS) + 2)
                    sp.wait_ge(ex_dlo, e - SLOTS + 1)
                slot = raw_ex[:, e % SLOTS, :]
                sp.dma_start(slot[:, 0:I], ex_gate[e]).then_inc(ld_ex[e % 2], 16)
                sp.dma_start(slot[:, I:2 * I], ex_up[e]).then_inc(ld_ex[e % 2], 16)
                sp.dma_start(slot[:, 2 * I:RAW].rearrange("p (c h) -> p c h", c=NC),
                             ex_down[e].rearrange("(c p) h -> p c h", p=P)).then_inc(ld_ex[e % 2], 16)
            with sp.Fori(0, B) as b:
                sp.wait_ge(out_ready, b + 1)
                sp.dma_start(out[bass.ds(b, 1)].rearrange("b s h -> s (b h)"),
                             base[:, bass.ds(b, 1), :].rearrange("p b h -> p (b h)")).then_inc(st_out, 16)
            sp.wait_ge(st_out, 16 * B)

        @block.gpsimd
        def _(pool):
            pool.memset(ident[:, :], 0.0).then_inc(ident_zero, 1)
            pool.memset(ones[:, :], 1.0).then_inc(consts, 1)
            pool.wait_ge(ident_zero, 1)
            pool.affine_select(out=ident[:, :], in_=ident[:, :], compare_op=ALU.not_equal, fill=1.0,
                               base=0, pattern=[[-1, P]], channel_multiplier=1).then_inc(consts, 1)

            def split_down(raw, dst, hi_sem, lo_sem, n):
                src = raw[:, 2 * I:RAW].rearrange("p (c h) -> p c h", c=NC)
                d = dst.rearrange("p (c v h) -> p c v h", c=NC, v=2)
                pool.tensor_copy(d[:, :, 0, :], src).then_inc(hi_sem, 1)
                pool.wait_ge(hi_sem, n)
                pool.tensor_tensor(d[:, :, 1, :], src, f32(d[:, :, 0, :]), ALU.subtract).then_inc(lo_sem, 1)

            pool.wait_ge(sh_hi, 1)
            pool.tensor_tensor(wsh[:, I:2 * I], raw_sh[:, 0:I], f32(wsh[:, 0:I]), ALU.subtract).then_inc(sh_glo, 1)
            pool.wait_ge(ld_sh_down, 16)
            split_down(raw_sh[:, :], wsh[:, DOWN:SPLIT], sh_dhi, sh_dlo, 1)
            for e in range(E):
                pool.wait_ge(ld_ex[e % 2], 48 * (e // 2 + 1))
                split_down(raw_ex[:, e % SLOTS, :], wex[:, e * SPLIT + DOWN:(e + 1) * SPLIT],
                           ex_dhi, ex_dlo, e + 1)

            def stage(b, j):
                pool.tensor_copy(xst[:, j, :, :], f32(x1s[:, bass.ds(b, 1), :, :]).rearrange("p a v s -> p (a v) s")
                                 ).then_inc(xst_ready, 2)

            pool.wait_ge(x1lo_ready, NG)
            for j in range(2):
                stage(j, j)
            with pool.Fori(1, B // 2) as i:
                for j in range(2):
                    pool.wait_ge(up_done, 4 * i + (NU + 2 * j - 2))
                    stage(2 * i + j, j)

        @block.scalar
        def _(act):
            act.dma_start(b_nat[:, :, :], Bs.rearrange("e o r -> o e r")).then_inc(ld_b, 16)
            act.dma_start(a_sb[:, :], As.rearrange("e r c -> (e r) c")).then_inc(ld_a, 16)
            act.dma_start(bias[:, :], b_base.rearrange("(o a) -> o a", a=1)).then_inc(ld_bias, 16)
            act.wait_ge(rt_step, 3)
            act.activation(rt[:, 8:16], top8[:, :], ACT.Exp, bias=rt[:, 0:1],
                           accum_out=rt[:, 1:2]).then_inc(exp_done, 1)
            act.wait_ge(exp_done, 1)
            act.activation(rt[:, 24:25], rt[:, 8:9], ACT.Gelu_apprx_tanh).then_inc(gelu_table, 1)

            def copy_xT(g):
                act.wait_ge(xT_ps, g + 1)
                act.copy(xT[:, g * GB:(g + 1) * GB, :], bank[4 + g][:, :].rearrange("p (b s) -> p b s", b=GB)
                         ).then_inc(xT_ready, 1)

            def split_x1_hi(g):
                act.wait_ge(x1_ready, g + 1)
                act.copy(x1_hi(g), xn[:, g * GB:(g + 1) * GB, :]).then_inc(x1hi_ready, 1)

            copy_xT(0)
            copy_xT(1)
            act.wait_ge(ld_sh_gate, 16)
            act.copy(wsh[:, 0:I], raw_sh[:, 0:I]).then_inc(sh_hi, 1)
            copy_xT(2)
            split_x1_hi(0)
            act.wait_ge(ld_sh_up, 16)
            act.copy(wsh[:, 2 * I:3 * I], raw_sh[:, I:2 * I]).then_inc(sh_hi, 1)
            copy_xT(3)
            split_x1_hi(1)

            def gelu(t, q):
                act.wait_ge(gate_done, t + 1)
                if not (isinstance(t, int) and t < 2):
                    act.wait_ge(h_done, t - 1)
                act.activation(gelu_sb[q], gate_ps[q][:, :], ACT.Gelu_apprx_tanh).then_inc(gelu_done, 1)

            def hi_shared(t, q):
                act.wait_ge(h_done, t + 1)
                if not (isinstance(t, int) and t < 2):
                    act.wait_ge(down_done, t - 1)
                act.copy(hT_hi[:, q, :], h_sb[q]).then_inc(hi_done, 1)

            def hi_expert(t, q):
                act.wait_ge(hT_done, t - (NU - 1))
                act.wait_ge(down_done, t - 1)
                act.copy(hT_hi[:, q, :], bank[6 + q][:, :]).then_inc(hi_done, 1)

            def split_hi(g, c):
                half = c % 2
                e = 2 * g + c // 2
                act.wait_ge(ld_ex[c // 2], 48 * g + 48)
                act.copy(wex[:, bass.ds(e * SPLIT + 2 * half * I, I)],
                         raw_ex[:, bass.ds(e % SLOTS, 1), half * I:(half + 1) * I].rearrange("p a n -> p (a n)")
                         ).then_inc(ex_hi, 1)

            def base_copy(g):
                act.wait_ge(sumT_done, g + 1)
                act.copy(base[:, bass.ds(g * GB, GB), :],
                         bank[5][:, :].rearrange("p (b s) -> p b s", b=GB)).then_inc(base_done, 1)

            def shared_group(g):
                for c in range(NC):
                    t = NC * g + c
                    gelu(t, c % 2)
                    if not (isinstance(t, int) and t == 0):
                        hi_shared(t - 1, (c + 1) % 2)
                    split_hi(g, c)
                    if c < 2 and isinstance(g, int) and g == 0:
                        split_x1_hi(2 + c)
                    if c == 3 and not (isinstance(g, int) and g == 0):
                        base_copy(g - 1)

            shared_group(0)
            with act.Fori(1, NG) as g:
                shared_group(g)
            for n in range(4):
                gelu(NU + n, n % 2)
                if n == 0:
                    hi_shared(NU - 1, 1)
                else:
                    hi_expert(NU + n - 1, (n + 1) % 2)
                if n == 2:
                    base_copy(NG - 1)
            with act.Fori(4, NE - 3, 4) as n0:
                for n in range(4):
                    gelu(n0 + (NU + n), n % 2)
                    hi_expert(n0 + (NU + n - 1), (n + 1) % 2)
            hi_expert(NU + NE - 1, 1)

        @block.vector
        def _(dve):
            dve.wait_ge(ld_cond, 16)
            dve.tensor_scalar(cond_er[:, :, :], cond_sb[:, :].rearrange("b (e a) -> b e a", a=1).to_broadcast([B, E, R]),
                              LORA_SCALING, None, ALU.mult).then_inc(cond_er_ready, 1)
            dve.max(top8[:, :], cond_sb[:, :]).then_inc(rt_step, 1)
            dve.wait_ge(rt_step, 1)
            dve.max_index(top_idx[:, :], top8[:, :], cond_sb[:, :]).then_inc(rt_step, 1)
            dve.tensor_scalar(rt[:, 0:1], top8[:, 0:1], -1.0, None, ALU.mult).then_inc(rt_step, 1)

            def rest_of_router():
                dve.wait_ge(exp_done, 1)
                dve.reciprocal(rt[:, 2:3], rt[:, 1:2]).then_inc(rt_step, 1)
                dve.wait_ge(rt_step, 4)
                dve.tensor_scalar(rt[:, 16:18], rt[:, 8:10], rt[:, 2:3], None, ALU.mult).then_inc(rt_step, 1)
                dve.wait_ge(rt_step, 5)
                dve.tensor_tensor(rt[:, 3:4], rt[:, 16:17], rt[:, 17:18], ALU.add).then_inc(rt_step, 1)
                dve.wait_ge(rt_step, 6)
                dve.reciprocal(rt[:, 4:5], rt[:, 3:4]).then_inc(rt_step, 1)
                dve.wait_ge(rt_step, 7)
                dve.tensor_scalar(rt[:, 18:20], rt[:, 16:18], rt[:, 4:5], None, ALU.mult).then_inc(rt_step, 1)
                dve.wait_ge(rt_step, 8)
                dve.tensor_scalar(rt[:, 20:22], rt[:, 18:20], GRAD_SCALE, None, ALU.mult).then_inc(rt_step, 1)
                dve.wait_ge(rt_step, 9)
                dve.scalar_tensor_tensor(rt[:, 22:24], rt[:, 18:20], 1.0 - GRAD_SCALE, rt[:, 20:22],
                                         ALU.mult, ALU.add).then_inc(rt_step, 1)
                dve.tensor_copy(top_idxf[:, :], top_idx[:, 0:2]).then_inc(rt_step, 1)
                dve.wait_ge(consts, 2)
                dve.wait_ge(rt_step, 11)
                for k in range(2):
                    dve.tensor_scalar(rdiag[:, k, :], ident[0:B, 0:B], rt[:, 22 + k:23 + k], None,
                                      ALU.mult).then_inc(rt_step, 1)
                for k in range(2):
                    dve.tensor_scalar(rdiag[:, 2 + k, :], ident[0:B, 0:B], top_idxf[:, k:k + 1], float(SPLIT),
                                      ALU.mult, ALU.mult).then_inc(rt_step, 1)

            def scale_B(g):
                if g >= 2:
                    dve.wait_ge(delta_ps, g - 1)
                dve.tensor_tensor(sB[:, g % 2, :, :],
                                  bT[:, :].rearrange("p (a o) -> p a o", a=1).to_broadcast([P, GB, H]),
                                  lora_s[:, g * GB:(g + 1) * GB].rearrange("p (b a) -> p b a", a=1)
                                  .to_broadcast([P, GB, H]), ALU.mult).then_inc(sB_ready, 1)

            def w_eff(g):
                dve.wait_ge(delta_ps, g + 1)
                dve.tensor_tensor(work[:, g, :].rearrange("p (b o) -> p b o", b=GB),
                                  bank[g][:, :].rearrange("p (b o) -> p b o", b=GB),
                                  wT[:, :].rearrange("p (a o) -> p a o", a=1).to_broadcast([P, GB, H]),
                                  ALU.add).then_inc(weff_ready, 1)

            def first_layer(g):
                dve.wait_ge(x1_ps, g + 1)
                dve.wait_ge(xT_ready, g + 1)
                dve.scalar_tensor_tensor(xn[:, g * GB:(g + 1) * GB, :],
                                         bank[4 + g][:, :].rearrange("p (b s) -> p b s", b=GB), bias[:, 0:1],
                                         xT[:, g * GB:(g + 1) * GB, :], ALU.add, ALU.add).then_inc(x1_ready, 1)

            def split_x1_lo(g):
                dve.wait_ge(x1hi_ready, g + 1)
                dve.tensor_tensor(x1_lo(g), xn[:, g * GB:(g + 1) * GB, :], f32(x1_hi(g)),
                                  ALU.subtract).then_inc(x1lo_ready, 1)

            dve.wait_ge(setup_ps, 1)
            dve.tensor_copy(lora_s[:, :], bank[5][:, 0:B]).then_inc(setup_sb, 1)
            dve.wait_ge(setup_ps, 2)
            dve.tensor_copy(bT[:, :], bank[7][:, 0:H]).then_inc(setup_sb, 1)
            dve.wait_ge(setup_sb, 2)
            scale_B(0)
            scale_B(1)
            dve.wait_ge(setup_ps, 3)
            dve.tensor_copy(wT[:, :], bank[6][:, 0:H]).then_inc(setup_sb, 1)
            dve.wait_ge(setup_sb, 3)
            w_eff(0)
            scale_B(2)
            w_eff(1)
            scale_B(3)
            dve.wait_ge(ld_bias, 16)
            first_layer(0)
            w_eff(2)
            split_x1_lo(0)
            first_layer(1)
            w_eff(3)
            dve.wait_ge(sh_hi, 2)
            dve.tensor_tensor(wsh[:, 3 * I:4 * I], raw_sh[:, I:2 * I], f32(wsh[:, 2 * I:3 * I]),
                              ALU.subtract).then_inc(sh_lo, 1)
            first_layer(2)
            split_x1_lo(1)
            first_layer(3)
            rest_of_router()

            def router_result():
                dve.wait_ge(setup_ps, 4)
                dve.tensor_copy(wgt[:, :, :], bank[5][:, 0:2 * B].rearrange("p (k b) -> p k b", k=2)
                                ).then_inc(setup_sb, 1)
                dve.tensor_copy(eidx[:, :].rearrange("p (b k) -> p k b", k=2),
                                bank[5][0:1, 2 * B:4 * B].rearrange("p (k b) -> p k b", k=2)).then_inc(setup_sb, 1)

            def h_shared(t, q):
                dve.wait_ge(up_done, t + 1)
                dve.wait_ge(gelu_done, t + 1)
                if not (isinstance(t, int) and t < 2):
                    dve.wait_ge(lo_done, t - 1)
                dve.tensor_tensor(h_sb[q], up_ps[q][:, :], gelu_sb[q], ALU.mult).then_inc(h_done, 1)

            def h_expert(t, q, b, k):
                dve.wait_ge(up_done, t + 1)
                dve.wait_ge(gelu_done, t + 1)
                if isinstance(t, int) and t < NU + 2:
                    dve.wait_ge(lo_done, t - 1)
                dve.scalar_tensor_tensor(h_sb[q], up_ps[q][:, :], wgt[:, k, bass.ds(b, 1)], gelu_sb[q],
                                         ALU.mult, ALU.mult).then_inc(h_done, 1)

            def lo(t, q, src):
                dve.wait_ge(hi_done, t + 1)
                if not (isinstance(t, int) and t < 2):
                    dve.wait_ge(down_done, t - 1)
                dve.tensor_tensor(hT_lo[:, q, :], src, f32(hT_hi[:, q, :]), ALU.subtract).then_inc(lo_done, 1)

            def split_lo(g, c):
                half = c % 2
                e = 2 * g + c // 2
                dve.wait_ge(ex_hi, NC * g + (c + 1))
                dve.tensor_tensor(wex[:, bass.ds(e * SPLIT + (2 * half + 1) * I, I)],
                                  raw_ex[:, bass.ds(e % SLOTS, 1), half * I:(half + 1) * I].rearrange("p a n -> p (a n)"),
                                  f32(wex[:, bass.ds(e * SPLIT + 2 * half * I, I)]),
                                  ALU.subtract).then_inc(ex_lo, 1)

            def sum_group(g):
                dve.wait_ge(down_done, NC * g + NC)
                if not (isinstance(g, int) and g == 0):
                    dve.wait_ge(sumT_done, g)
                dve.tensor_tensor(s1T[:, :].rearrange("p (b s) -> p b s", b=GB),
                                  bank[4][:, :].rearrange("p (b s) -> p b s", b=GB),
                                  xn[:, bass.ds(g * GB, GB), :], ALU.add).then_inc(sum_done, 1)

            def shared_group(g):
                for c in range(NC):
                    t = NC * g + c
                    h_shared(t, c % 2)
                    if not (isinstance(t, int) and t == 0):
                        lo(t - 1, (c + 1) % 2, h_sb[(c + 1) % 2])
                    if c == 1 and not (isinstance(g, int) and g == 0):
                        sum_group(g - 1)
                    split_lo(g, c)
                    if c < 2 and isinstance(g, int) and g == 0:
                        split_x1_lo(2 + c)
                    if c == 3 and isinstance(g, int) and g == 0:
                        router_result()

            def result(b, j):
                of_b = base[:, bass.ds(b, 1), :].rearrange("p a h -> p (a h)")
                dve.wait_ge(down_done, 2 * b + (NU + 2))
                dve.tensor_tensor(of_b, bank[4 + j][:, 0:H], of_b, ALU.add).then_inc(acc_done, 1)
                dve.wait_ge(acc_done, b + 1)
                dve.tensor_tensor(of_b, bank[4 + j][:, H:2 * H], of_b, ALU.add).then_inc(out_ready, 1)

            shared_group(0)
            with dve.Fori(1, NG) as g:
                shared_group(g)
            dve.wait_ge(setup_sb, 5)
            for n in range(4):
                h_expert(NU + n, n % 2, n // 2, n % 2)
                if n == 0:
                    lo(NU - 1, 1, h_sb[1])
                else:
                    lo(NU + n - 1, (n + 1) % 2, bank[6 + (n + 1) % 2][:, :])
                if n == 1:
                    sum_group(NG - 1)
                if n == 3:
                    dve.wait_ge(base_done, NG)
                    result(0, 0)
            with dve.Fori(1, B // 2) as i:
                n0 = dve.snap(4 * i)
                for n in range(4):
                    h_expert(n0 + (NU + n), n % 2, 2 * i + n // 2, n % 2)
                    lo(n0 + (NU + n - 1), (n + 1) % 2, bank[6 + (n + 1) % 2][:, :])
                    if n == 1:
                        result(2 * i - 1, 1)
                    if n == 3:
                        result(2 * i, 0)
            lo(NU + NE - 1, 1, bank[7][:, :])
            result(B - 1, 1)

        @block.tensor
        def _(pe):
            pe.wait_ge(consts, 2)
            pe.wait_ge(cond_er_ready, 1)
            pe.transpose(bank[5][:, 0:B], cond_er[:, :, :].rearrange("b e r -> b (e r)"), ident[0:B, 0:B]
                         ).then_inc(setup_ps, 1)
            pe.wait_ge(ld_b, 16)
            pe.transpose(bank[7][:, 0:H], b_nat[:, :, :].rearrange("o e r -> o (e r)"), ident[:, :]
                         ).then_inc(setup_ps, 1)

            def x_transposes(g):
                pe.wait_ge(ld_x[g], 16)
                for j in range(GB):
                    mm = pe.transpose(bank[4 + g][:, j * S:(j + 1) * S], xn[:, g * GB + j, :], ident[:, :])
                mm.then_inc(xT_ps, 1)

            def delta_w(g):
                pe.wait_ge(sB_ready, g + 1)
                pe.matmul(bank[g][:, :], a_sb[:, :], sB[:, g % 2, :, :].rearrange("p b o -> p (b o)"),
                          start=True, stop=True).then_inc(delta_ps, 1)

            def first_layer(g):
                pe.wait_ge(weff_ready, g + 1)
                pe.wait_ge(xT_ready, g + 1)
                for j in range(GB):
                    mm = pe.matmul(bank[4 + g][:, j * S:(j + 1) * S], work[:, g, j * H:(j + 1) * H],
                                   xT[:, g * GB + j, :], start=True, stop=True)
                mm.then_inc(x1_ps, 1)

            x_transposes(0)
            pe.wait_ge(ld_w, 16)
            pe.transpose(bank[6][:, 0:H], w_nat[:, :], ident[:, :]).then_inc(setup_ps, 1)
            pe.wait_ge(ld_a, 16)
            delta_w(0)
            pe.wait_ge(setup_sb, 3)
            x_transposes(1)
            delta_w(1)
            first_layer(0)
            x_transposes(2)
            delta_w(2)
            first_layer(1)
            x_transposes(3)
            delta_w(3)
            first_layer(2)
            first_layer(3)

            def gate_up_shared(g, c):
                q = c % 2
                t = NC * g + c
                if isinstance(t, int) and t < 2:
                    pe.wait_ge(weff_ready, 2 * t + 2)
                elif isinstance(t, int) and t < 4:
                    pe.wait_ge(h_done, t - 1)
                if c == 0:
                    pe.wait_ge(x1lo_ready, g + 1)
                for first, ps, done in ((G_HI, gate_ps[q], gate_done), (U_HI, up_ps[q], up_done)):
                    w_hi = wsh[:, first + c * P:first + (c + 1) * P]
                    w_lo = wsh[:, first + I + c * P:first + I + (c + 1) * P]
                    pe.matmul(ps[:, :], w_hi, x1_hi(g), start=True, stop=False)
                    pe.matmul(ps[:, :], w_hi, x1_lo(g), start=False, stop=False)
                    pe.matmul(ps[:, :], w_lo, x1_hi(g), start=False, stop=True).then_inc(done, 1)

            def down_shared(g, c):
                q = c % 2
                pe.wait_ge(lo_done, NC * g + (c + 1))
                if c == 0:
                    if isinstance(g, int) and g == 0:
                        pe.wait_ge(x1_ready, 1)
                        pe.wait_ge(sh_dlo, 1)
                    else:
                        pe.wait_ge(sum_done, g)
                w_hi = wsh[:, DOWN + 2 * c * H:DOWN + (2 * c + 1) * H]
                w_lo = wsh[:, DOWN + (2 * c + 1) * H:DOWN + (2 * c + 2) * H]
                pe.matmul(bank[4][:, :], w_hi, hT_hi[:, q, :], start=(c == 0), stop=False)
                pe.matmul(bank[4][:, :], w_hi, hT_lo[:, q, :], start=False, stop=False)
                pe.matmul(bank[4][:, :], w_lo, hT_hi[:, q, :], start=False, stop=(c == NC - 1)
                          ).then_inc(down_done, 1)

            def sum_transposes(g):
                pe.wait_ge(sum_done, g + 1)
                if not (isinstance(g, int) and g == 0):
                    pe.wait_ge(base_done, g)
                for j in range(GB):
                    mm = pe.transpose(bank[5][:, j * H:(j + 1) * H], s1T[:, j * S:(j + 1) * S], ident[:, :])
                mm.then_inc(sumT_done, 1)

            def shared_group(g):
                first = isinstance(g, int) and g == 0
                for c in range(NC):
                    gate_up_shared(g, c)
                    if c >= 2:
                        down_shared(g, c - 2)
                    elif not first:
                        down_shared(g - 1, c + 2)
                    if c == 2 and not first:
                        sum_transposes(g - 1)
                    if c == 2 and first:
                        pe.wait_ge(rt_step, 15)
                        pe.wait_ge(x1_ready, 2)
                        pe.matmul(bank[5][:, 0:4 * B], ones[:, :], rdiag[:, :, :].rearrange("p k b -> p (k b)"),
                                  start=True, stop=True).then_inc(setup_ps, 1)

            def weights_of(n):
                return pe.value_load(eidx[0:1, bass.ds(n, 1)], min_val=0, max_val=(E - 1) * SPLIT)

            def gate_up_expert(q, j, w0):
                for first, ps, done in ((G_HI, gate_ps[q], gate_done), (U_HI, up_ps[q], up_done)):
                    w_hi = wex[:, bass.ds(w0 + first, I)]
                    w_lo = wex[:, bass.ds(w0 + (first + I), I)]
                    pe.matmul(ps[:, :], xst[:, j, 0, :], w_hi, start=True, stop=False)
                    pe.matmul(ps[:, :], xst[:, j, 1, :], w_hi, start=False, stop=False)
                    pe.matmul(ps[:, :], xst[:, j, 0, :], w_lo, start=False, stop=True).then_inc(done, 1)

            def h_transposes(n, q):
                pe.wait_ge(h_done, n + (NU + 1))
                for c in range(NC):
                    mm = pe.transpose(bank[6 + q][:, c * P:(c + 1) * P], h_sb[q][:, c * P:(c + 1) * P], ident[:, :])
                mm.then_inc(hT_done, 1)

            def down_expert(n, q, k, j, w0):
                pe.wait_ge(lo_done, n + (NU + 1))
                for c in range(NC):
                    w = wex[:, bass.ds(w0 + (DOWN + 2 * c * H), 2 * H)]
                    pe.matmul(bank[4 + j][:, 0:2 * H], hT_hi[:, q, c * P:(c + 1) * P], w,
                              start=(k == 0 and c == 0), stop=False)
                    mm = pe.matmul(bank[4 + j][:, 0:2 * H], hT_lo[:, q, c * P:(c + 1) * P], w,
                                   start=False, stop=(k == 1 and c == NC - 1))
                mm.then_inc(down_done, 1)

            pe.wait_ge(sh_glo, 1)
            pe.wait_ge(sh_lo, 1)
            shared_group(0)
            with pe.Fori(1, NG) as g:
                shared_group(g)
            down_shared(NG - 1, NC - 2)
            pe.wait_ge(setup_sb, 5)
            w_at = [weights_of(n) for n in range(4)]
            pe.wait_ge(ex_lo, 2 * E)
            pe.wait_ge(ex_dlo, E)
            for n in range(4):
                if n % 2 == 0:
                    pe.wait_ge(xst_ready, n + 2)
                gate_up_expert(n % 2, n // 2, w_at[n])
                if n >= 1:
                    h_transposes(n - 1, (n + 1) % 2)
                if n == 1:
                    down_shared(NG - 1, NC - 1)
                if n == 2:
                    sum_transposes(NG - 1)
                if n >= 2:
                    down_expert(n - 2, n % 2, n % 2, 0, w_at[n - 2])
            pe.wait_ge(base_done, NG)
            with pe.Fori(4, NE - 3, 4) as n0:
                w_at = {}
                for n in range(4):
                    w_at[n] = weights_of(n0 + n)
                    if n % 2 == 0:
                        pe.wait_ge(xst_ready, n0 + (n + 2))
                    gate_up_expert(n % 2, n // 2, w_at[n])
                    if n < 2:
                        w_at[n - 2] = weights_of(n0 + (n - 2))
                    h_transposes(n0 + (n - 1), (n + 1) % 2)
                    down_expert(n0 + (n - 2), n % 2, n % 2, (n // 2 + 1) % 2, w_at[n - 2])
            w_at = [weights_of(NE - 2), weights_of(NE - 1)]
            h_transposes(NE - 1, 1)
            down_expert(NE - 2, 0, 0, 1, w_at[0])
            down_expert(NE - 1, 1, 1, 1, w_at[1])


_INS = ["x", "cond_8", "L0_cond_W_base", "L0_cond_b_base", "L0_cond_As", "L0_cond_Bs",
        "L1_cond_skill_gate", "L1_cond_skill_up", "L1_cond_skill_down",
        "L1_cond_shared_gate", "L1_cond_shared_up", "L1_cond_shared_down"]
_OUTS = [((16, 128, 128), "float32")]


def kernel(**inputs):
    import numpy as _np
    import concourse.bacc as _bacc
    from concourse import mybir as _mybir
    from concourse.bass_utils import run_bass_kernel_spmd as _run

    nc = _bacc.Bacc("TRN2", target_bir_lowering=False, num_devices=1)
    arrays, args = {}, []
    for name in _INS:
        a = _np.ascontiguousarray(inputs[name])
        arrays[f"in_{name}_dram"] = a
        args.append(nc.dram_tensor(f"in_{name}_dram", a.shape, _mybir.dt.from_np(a.dtype), kind="ExternalInput").ap())
    for i, (shape, dtype) in enumerate(_OUTS):
        dt = _mybir.dt.from_np(_np.dtype(dtype))
        args.append(nc.dram_tensor(f"out_{i}_dram", shape, dt, kind="ExternalOutput").ap())
    lora_then_top2_moe(nc, *args)
    r = _run(nc, [arrays], core_ids=[0])
    return r.results[0]["out_0_dram"]
```

```python
from contextlib import ExitStack

import concourse.bass as bass
from concourse import mybir

F32 = mybir.dt.float32
F32R = mybir.dt.float32r
U32 = mybir.dt.uint32
I32 = mybir.dt.int32
ALU = mybir.AluOpType
ACT = mybir.ActivationFunctionType

LORA_SCALING = 2.0
GRAD_SCALE = 1.0 / 12.0


def lora_then_top2_moe(nc, x, cond, W_base, b_base, As, Bs, ex_gate, ex_up, ex_down,
                       sh_gate, sh_up, sh_down, out):
    B, S, H = x.shape
    E, _, I = ex_gate.shape
    R = As.shape[1]
    P = 128
    assert S == P and H == P and E * R == P and I == 512
    GB = I // S
    NG = B // GB
    NC = I // P
    WARM_UP = 5
    DN = NC * H
    GU = 4 * I
    G_HI, U_HI = 0, 2 * I

    with ExitStack() as ctx:
        def sb(name, shape, dt=F32):
            return ctx.enter_context(nc.sbuf_tensor(name, shape, dt))

        def sem(name):
            return ctx.enter_context(nc.semaphore(name))

        cond_sb = sb("cond_sb", [B, E])
        a_sb = sb("a_sb", [P, H])
        b_nat = sb("b_nat", [H, E, R])
        w_nat = sb("w_nat", [H, H])
        bias = sb("bias", [H, 1])
        ident = sb("ident", [P, P])
        ones = sb("ones", [B, P])
        zeros = sb("zeros", [P, P])
        bT = sb("bT", [P, H])
        wT = sb("wT", [H, H])
        cond_er = sb("cond_er", [B, E, R])
        lora_s = sb("lora_s", [P, B])
        top8 = sb("top8", [B, 8])
        top_idx = sb("top_idx", [B, 8], U32)
        top_idxf = sb("top_idxf", [B, 2])
        rt = sb("rt", [B, 32])
        rdiag = sb("rdiag", [B, 4, B])
        wgt = sb("wgt", [P, 2, B])
        eidx = sb("eidx", [1, 2 * B], I32)

        xn = sb("xn", [P, B, H])
        xT = sb("xT", [P, B, S])
        sB = sb("sB", [P, 2, GB, H])
        work = sb("work", [P, 4, I])
        x1s = sb("x1s", [P, B, 2, S], F32R)
        s1T = sb("s1T", [P, I])
        raw_sh = sb("raw_sh", [P, 2, I])
        raw_shd = sb("raw_shd", [P, NC, H])
        raw_ex = sb("raw_ex", [P, E, 2, I])
        wsh = sb("wsh", [P, GU], F32R)
        wshd = sb("wshd", [P, 2, NC, H], F32R)
        wex = sb("wex", [P, E * GU], F32R)
        wexd = sb("wexd", [P, E * DN])
        hT_hi = sb("hT_hi", [P, 2, I], F32R)
        hT_lo = sb("hT_lo", [P, 2, I], F32R)
        hT = sb("hT", [P, 2, I])
        xst = sb("xst", [P, 2, 2, S], F32R)

        def f32(ap):
            return ap.bitcast(F32)

        bank = [ctx.enter_context(nc.psum_tensor(f"bank{i}", [P, I], F32)) for i in range(8)]
        gate_ps = [bank[0], bank[2]]
        up_ps = [bank[1], bank[3]]

        ld_cond, ld_a, ld_b, ld_w, ld_bias = [sem(f"ld_{n}") for n in ("cond", "a", "b", "w", "bias")]
        ld_x = [sem(f"ld_x{g}") for g in range(NG)]
        ld_sh_gate = sem("ld_sh_gate")
        ld_sh_up = sem("ld_sh_up")
        ld_sh_down = sem("ld_sh_down")
        ld_down = sem("ld_down")
        ld_ex = [sem("ld_ex_even"), sem("ld_ex_odd")]
        zeros_ready = sem("zeros_ready")
        consts = sem("consts")
        ident_zero = sem("ident_zero")
        rt_step = sem("rt_step")
        exp_done = sem("exp_done")
        cond_er_ready = sem("cond_er_ready")
        setup_ps = sem("setup_ps")
        setup_sb = sem("setup_sb")
        sB_ready = sem("sB_ready")
        xT_ps = sem("xT_ps")
        xT_ready = sem("xT_ready")
        delta_ps = sem("delta_ps")
        weff_ready = sem("weff_ready")
        x1_ps = sem("x1_ps")
        x1_ready = sem("x1_ready")
        x1hi_ready = sem("x1hi_ready")
        x1lo_first = sem("x1lo_first")
        x1lo_later = sem("x1lo_later")
        sh_hi = sem("sh_hi")
        sh_lo = sem("sh_lo")
        sh_glo = sem("sh_glo")
        sh_dhi = sem("sh_dhi")
        sh_dlo = sem("sh_dlo")
        ex_hi = sem("ex_hi")
        ex_glo = sem("ex_glo")
        ex_ulo = sem("ex_ulo")
        gate_done = sem("gate_done")
        up_done = sem("up_done")
        gelu_done = sem("gelu_done")
        h_done = sem("h_done")
        hT_done = sem("hT_done")
        hT_ready = sem("hT_ready")
        hi_done = sem("hi_done")
        lo_done = sem("lo_done")
        down_done = sem("down_done")
        sum_done = sem("sum_done")
        sumT_done = sem("sumT_done")
        base_done = sem("base_done")
        xst_ready = sem("xst_ready")
        out_ready = sem("out_ready")
        st_out = sem("st_out")

        gelu_sb = [work[:, 0, :], work[:, 1, :]]
        h_sb = [work[:, 2, :], work[:, 3, :]]
        base = xT

        def x1_hi(g):
            return x1s[:, bass.ds(g * GB, GB), 0, :]

        def x1_lo(g):
            return x1s[:, bass.ds(g * GB, GB), 1, :]

        NU = NG * NC
        NE = 2 * B

        block = ctx.enter_context(nc.Block())

        @block.sync
        def _(sp):
            sp.dma_start(b_nat[:, :, :], Bs.rearrange("e o r -> o e r")).then_inc(ld_b, 16)
            sp.dma_start(xn[:, 0:GB, :], x[0:GB].rearrange("b s h -> s b h")).then_inc(ld_x[0], 16)
            sp.dma_start(w_nat[:, :], W_base).then_inc(ld_w, 16)

            def load_x(g):
                sp.dma_start(xn[:, g * GB:(g + 1) * GB, :],
                             x[g * GB:(g + 1) * GB].rearrange("b s h -> s b h")).then_inc(ld_x[g], 16)

            load_x(1)
            sp.dma_start(raw_sh[:, 0, :], sh_gate).then_inc(ld_sh_gate, 16)
            load_x(2)
            sp.dma_start(raw_sh[:, 1, :], sh_up).then_inc(ld_sh_up, 16)
            load_x(3)
            sp.dma_start(raw_shd[:, :, :], sh_down.rearrange("(c p) h -> p c h", p=P)).then_inc(ld_sh_down, 16)
            for e in range(E):
                if e >= 2:
                    sp.wait_ge(ld_ex[e % 2], 32 * (e // 2))
                sp.dma_start(raw_ex[:, e, 0, :], ex_gate[e]).then_inc(ld_ex[e % 2], 16)
                sp.dma_start(raw_ex[:, e, 1, :], ex_up[e]).then_inc(ld_ex[e % 2], 16)
            for half in range(2):
                e0 = half * E // 2
                sp.dma_start(wexd[:, e0 * DN:(e0 + E // 2) * DN].rearrange("p (n h) -> p n h", h=H),
                             ex_down[e0:e0 + E // 2].rearrange("e (c p) h -> p (e c) h", p=P)).then_inc(ld_down, 16)
            with sp.Fori(0, B) as b:
                sp.wait_ge(out_ready, b + 1)
                sp.dma_start(out[bass.ds(b, 1)].rearrange("b s h -> s (b h)"),
                             base[:, bass.ds(b, 1), :].rearrange("p b h -> p (b h)")).then_inc(st_out, 16)
            sp.wait_ge(st_out, 16 * B)

        @block.gpsimd
        def _(pool):
            pool.memset(ident[:, :], 0.0).then_inc(ident_zero, 1)
            pool.memset(ones[:, :], 1.0).then_inc(consts, 1)
            pool.wait_ge(ident_zero, 1)
            pool.affine_select(out=ident[:, :], in_=ident[:, :], compare_op=ALU.not_equal, fill=1.0,
                               base=0, pattern=[[-1, P]], channel_multiplier=1).then_inc(consts, 1)

            pool.wait_ge(sh_hi, 1)
            pool.tensor_tensor(wsh[:, I:2 * I], raw_sh[:, 0, :], f32(wsh[:, 0:I]), ALU.subtract).then_inc(sh_glo, 1)
            pool.wait_ge(ld_sh_down, 16)
            pool.tensor_copy(wshd[:, 0, :, :], raw_shd[:, :, :]).then_inc(sh_dhi, 1)
            pool.wait_ge(sh_dhi, 1)
            pool.tensor_tensor(wshd[:, 1, :, :], raw_shd[:, :, :], f32(wshd[:, 0, :, :]), ALU.subtract).then_inc(sh_dlo, 1)
            for g in range(1, NG):
                if g >= 2:
                    pool.wait_ge(x1_ready, g + 1)
                    pool.tensor_copy(x1_hi(g), xn[:, g * GB:(g + 1) * GB, :]).then_inc(x1hi_ready, 1)
                pool.wait_ge(x1hi_ready, g + 1)
                pool.tensor_tensor(x1_lo(g), xn[:, g * GB:(g + 1) * GB, :], f32(x1_hi(g)),
                                   ALU.subtract).then_inc(x1lo_later, 1)
            def stage(b, j):
                pool.tensor_copy(xst[:, j, :, :], f32(x1s[:, bass.ds(b, 1), :, :]).rearrange("p a v s -> p (a v) s")
                                 ).then_inc(xst_ready, 2)

            pool.wait_ge(x1lo_first, 1)
            pool.wait_ge(x1lo_later, NG - 1)
            for j in range(2):
                stage(j, j)
            with pool.Fori(0, E) as e:
                pool.wait_ge(ex_hi, 2 * e + 2)
                pool.tensor_tensor(wex[:, bass.ds(e * GU + U_HI + I, I)],
                                   raw_ex[:, bass.ds(e, 1), 1, :].rearrange("p a n -> p (a n)"),
                                   f32(wex[:, bass.ds(e * GU + U_HI, I)]), ALU.subtract).then_inc(ex_ulo, 1)
            with pool.Fori(1, B // 2) as i:
                for j in range(2):
                    pool.wait_ge(up_done, 4 * i + (NU + 2 * j - 2))
                    stage(2 * i + j, j)

        @block.scalar
        def _(act):
            act.dma_start(cond_sb[:, :], cond).then_inc(ld_cond, 16)
            act.dma_start(a_sb[:, :], As.rearrange("e r c -> (e r) c")).then_inc(ld_a, 16)
            act.dma_start(bias[:, :], b_base.rearrange("(o a) -> o a", a=1)).then_inc(ld_bias, 16)
            act.wait_ge(rt_step, 3)
            act.activation(rt[:, 8:16], top8[:, :], ACT.Exp, bias=rt[:, 0:1],
                           accum_out=rt[:, 1:2]).then_inc(exp_done, 1)
            def copy_xT(g):
                act.wait_ge(xT_ps, g + 1)
                act.copy(xT[:, g * GB:(g + 1) * GB, :], bank[4 + g][:, :].rearrange("p (b s) -> p b s", b=GB)
                         ).then_inc(xT_ready, 1)

            def split_x1_hi(g):
                act.wait_ge(x1_ready, g + 1)
                act.copy(x1_hi(g), xn[:, g * GB:(g + 1) * GB, :]).then_inc(x1hi_ready, 1)

            act.wait_ge(exp_done, 1)
            copy_xT(0)
            copy_xT(1)
            act.wait_ge(ld_sh_gate, 16)
            act.copy(wsh[:, 0:I], raw_sh[:, 0, :]).then_inc(sh_hi, 1)
            copy_xT(2)
            split_x1_hi(0)
            act.wait_ge(ld_sh_up, 16)
            act.copy(wsh[:, 2 * I:3 * I], raw_sh[:, 1, :]).then_inc(sh_hi, 1)
            copy_xT(3)
            split_x1_hi(1)
            act.activation(rt[:, 24:25], rt[:, 8:9], ACT.Gelu_apprx_tanh)

            def gelu(t, q):
                act.wait_ge(gate_done, t + 1)
                if not (isinstance(t, int) and t < 2):
                    act.wait_ge(h_done, t - 1)
                act.activation(gelu_sb[q], gate_ps[q][:, :], ACT.Gelu_apprx_tanh).then_inc(gelu_done, 1)

            def hi_shared(t, q):
                act.wait_ge(h_done, t + 1)
                if not (isinstance(t, int) and t < 2):
                    act.wait_ge(down_done, t - 1)
                act.copy(hT_hi[:, q, :], h_sb[q]).then_inc(hi_done, 1)

            def copy_hT(t, q):
                act.wait_ge(hT_done, t - (NU - 1))
                if not (isinstance(t, int) and t < NU + 2):
                    act.wait_ge(down_done, t - 1)
                act.copy(hT[:, q, :], bank[6 + q][:, :]).then_inc(hT_ready, 1)

            def split_hi(g, c):
                half = c % 2
                e = 2 * g + c // 2
                act.wait_ge(ld_ex[c // 2], 32 * g + 32)
                act.copy(wex[:, bass.ds(e * GU + half * U_HI, I)],
                         raw_ex[:, bass.ds(e, 1), half, :].rearrange("p a n -> p (a n)")).then_inc(ex_hi, 1)

            def base_copy(g):
                act.wait_ge(sumT_done, g + 1)
                act.copy(base[:, bass.ds(g * GB, GB), :],
                         bank[5][:, :].rearrange("p (b s) -> p b s", b=GB)).then_inc(base_done, 1)

            def shared_group(g):
                for c in range(NC):
                    t = NC * g + c
                    first = isinstance(g, int) and g == 0
                    if not first or c == 0:
                        split_hi(g, c)
                    if c == 1:
                        hi_shared(t - 1, 0)
                    gelu(t, c % 2)
                    if c > 1 or (c == 0 and not first):
                        hi_shared(t - 1, (c + 1) % 2)
                    if first and c > 0:
                        split_hi(g, c)
                    if c == 3 and not first:
                        base_copy(g - 1)

            shared_group(0)
            with act.Fori(1, NG) as g:
                shared_group(g)
            for n in range(4):
                gelu(NU + n, n % 2)
                if n == 0:
                    hi_shared(NU - 1, 1)
                else:
                    copy_hT(NU + n - 1, (n + 1) % 2)
                if n == 2:
                    base_copy(NG - 1)
            with act.Fori(4, NE - 3, 4) as n0:
                for n in range(4):
                    gelu(n0 + (NU + n), n % 2)
                    copy_hT(n0 + (NU + n - 1), (n + 1) % 2)
            copy_hT(NU + NE - 1, 1)

        @block.vector
        def _(dve):
            dve.memset(zeros[:, :], 0.0).then_inc(zeros_ready, 1)
            dve.wait_ge(ld_cond, 16)
            dve.tensor_scalar(cond_er[:, :, :], cond_sb[:, :].rearrange("b (e a) -> b e a", a=1).to_broadcast([B, E, R]),
                              LORA_SCALING, None, ALU.mult).then_inc(cond_er_ready, 1)
            dve.max(top8[:, :], cond_sb[:, :]).then_inc(rt_step, 1)
            dve.wait_ge(rt_step, 1)
            dve.max_index(top_idx[:, :], top8[:, :], cond_sb[:, :]).then_inc(rt_step, 1)
            dve.tensor_scalar(rt[:, 0:1], top8[:, 0:1], -1.0, None, ALU.mult).then_inc(rt_step, 1)

            def router_weights():
                dve.wait_ge(exp_done, 1)
                dve.reciprocal(rt[:, 2:3], rt[:, 1:2]).then_inc(rt_step, 1)
                dve.wait_ge(rt_step, 4)
                dve.tensor_scalar(rt[:, 16:18], rt[:, 8:10], rt[:, 2:3], None, ALU.mult).then_inc(rt_step, 1)
                dve.wait_ge(rt_step, 5)
                dve.tensor_tensor(rt[:, 3:4], rt[:, 16:17], rt[:, 17:18], ALU.add).then_inc(rt_step, 1)
                dve.wait_ge(rt_step, 6)
                dve.reciprocal(rt[:, 4:5], rt[:, 3:4]).then_inc(rt_step, 1)
                dve.wait_ge(rt_step, 7)
                dve.tensor_scalar(rt[:, 18:20], rt[:, 16:18], rt[:, 4:5], None, ALU.mult).then_inc(rt_step, 1)
                dve.wait_ge(rt_step, 8)
                dve.tensor_scalar(rt[:, 20:22], rt[:, 18:20], GRAD_SCALE, None, ALU.mult).then_inc(rt_step, 1)
                dve.wait_ge(rt_step, 9)
                dve.scalar_tensor_tensor(rt[:, 22:24], rt[:, 18:20], 1.0 - GRAD_SCALE, rt[:, 20:22],
                                         ALU.mult, ALU.add).then_inc(rt_step, 1)
                dve.tensor_copy(top_idxf[:, :], top_idx[:, 0:2]).then_inc(rt_step, 1)

            def router_diagonals():
                dve.wait_ge(consts, 2)
                dve.wait_ge(rt_step, 11)
                for k in range(2):
                    dve.tensor_scalar(rdiag[:, k, :], ident[0:B, 0:B], rt[:, 22 + k:23 + k], None,
                                      ALU.mult).then_inc(rt_step, 1)
                for k in range(2):
                    dve.tensor_scalar(rdiag[:, 2 + k, :], ident[0:B, 0:B], top_idxf[:, k:k + 1], float(DN),
                                      ALU.mult, ALU.mult).then_inc(rt_step, 1)

            def scale_B(g, bT=bT):
                if g >= 2:
                    dve.wait_ge(delta_ps, g - 1)
                dve.tensor_tensor(sB[:, g % 2, :, :],
                                  bT[:, :].rearrange("p (a o) -> p a o", a=1).to_broadcast([P, GB, H]),
                                  lora_s[:, g * GB:(g + 1) * GB].rearrange("p (b a) -> p b a", a=1)
                                  .to_broadcast([P, GB, H]), ALU.mult).then_inc(sB_ready, 1)

            def w_eff(g):
                dve.wait_ge(delta_ps, g + 1)
                dve.tensor_tensor(work[:, g, :].rearrange("p (b o) -> p b o", b=GB),
                                  bank[g][:, :].rearrange("p (b o) -> p b o", b=GB),
                                  wT[:, :].rearrange("p (a o) -> p a o", a=1).to_broadcast([P, GB, H]),
                                  ALU.add).then_inc(weff_ready, 1)

            def first_layer(g):
                dve.wait_ge(x1_ps, g + 1)
                dve.wait_ge(xT_ready, g + 1)
                dve.scalar_tensor_tensor(xn[:, g * GB:(g + 1) * GB, :],
                                         bank[4 + g][:, :].rearrange("p (b s) -> p b s", b=GB), bias[:, 0:1],
                                         xT[:, g * GB:(g + 1) * GB, :], ALU.add, ALU.add).then_inc(x1_ready, 1)

            dve.wait_ge(setup_ps, 1)
            dve.tensor_copy(lora_s[:, :], bank[5][:, 0:B]).then_inc(setup_sb, 1)
            dve.wait_ge(setup_ps, 2)
            dve.wait_ge(setup_sb, 1)
            scale_B(0, bank[7][:, 0:H])
            dve.tensor_copy(bT[:, :], bank[7][:, 0:H]).then_inc(setup_sb, 1)
            dve.wait_ge(setup_sb, 2)
            scale_B(1)
            dve.wait_ge(setup_ps, 3)
            dve.tensor_copy(wT[:, :], bank[6][:, 0:H]).then_inc(setup_sb, 1)
            router_weights()
            dve.wait_ge(setup_sb, 3)
            w_eff(0)
            scale_B(2)
            router_diagonals()
            w_eff(1)
            scale_B(3)
            dve.wait_ge(ld_bias, 16)
            first_layer(0)
            w_eff(2)
            dve.wait_ge(x1hi_ready, 1)
            dve.tensor_tensor(x1_lo(0), xn[:, 0:GB, :], f32(x1_hi(0)), ALU.subtract).then_inc(x1lo_first, 1)
            first_layer(1)
            w_eff(3)
            dve.wait_ge(sh_hi, 2)
            dve.tensor_tensor(wsh[:, 3 * I:4 * I], raw_sh[:, 1, :], f32(wsh[:, 2 * I:3 * I]),
                              ALU.subtract).then_inc(sh_lo, 1)
            first_layer(2)
            first_layer(3)
            dve.wait_ge(setup_ps, 4)
            dve.tensor_copy(wgt[:, :, :], bank[5][:, 0:2 * B].rearrange("p (k b) -> p k b", k=2)
                            ).then_inc(setup_sb, 1)
            dve.tensor_copy(eidx[:, :].rearrange("p (b k) -> p k b", k=2),
                            bank[5][0:1, 2 * B:4 * B].rearrange("p (k b) -> p k b", k=2)).then_inc(setup_sb, 1)

            def h_shared(t, q):
                dve.wait_ge(up_done, t + 1)
                dve.wait_ge(gelu_done, t + 1)
                if not (isinstance(t, int) and t < 2):
                    dve.wait_ge(lo_done, t - 1)
                dve.tensor_tensor(h_sb[q], up_ps[q][:, :], gelu_sb[q], ALU.mult).then_inc(h_done, 1)

            def h_expert(t, q, b, k):
                dve.wait_ge(up_done, t + 1)
                dve.wait_ge(gelu_done, t + 1)
                if isinstance(t, int) and t < NU + 2:
                    dve.wait_ge(lo_done, t - 1)
                dve.scalar_tensor_tensor(h_sb[q], up_ps[q][:, :], wgt[:, k, bass.ds(b, 1)], gelu_sb[q],
                                         ALU.mult, ALU.mult).then_inc(h_done, 1)

            def lo_shared(t, q):
                dve.wait_ge(hi_done, t + 1)
                if not (isinstance(t, int) and t < 2):
                    dve.wait_ge(down_done, t - 1)
                dve.tensor_tensor(hT_lo[:, q, :], h_sb[q], f32(hT_hi[:, q, :]), ALU.subtract).then_inc(lo_done, 1)

            def split_gate_lo(g, c):
                e = 2 * g + c // 2
                dve.wait_ge(ex_hi, NC * g + (c + 1))
                dve.tensor_tensor(wex[:, bass.ds(e * GU + I, I)],
                                  raw_ex[:, bass.ds(e, 1), 0, :].rearrange("p a n -> p (a n)"),
                                  f32(wex[:, bass.ds(e * GU, I)]), ALU.subtract).then_inc(ex_glo, 1)

            def sum_group(g):
                dve.wait_ge(down_done, NC * g + NC)
                if not (isinstance(g, int) and g == 0):
                    dve.wait_ge(sumT_done, g)
                dve.tensor_tensor(s1T[:, :].rearrange("p (b s) -> p b s", b=GB),
                                  bank[4][:, :].rearrange("p (b s) -> p b s", b=GB),
                                  xn[:, bass.ds(g * GB, GB), :], ALU.add).then_inc(sum_done, 1)

            def shared_group(g):
                for c in range(NC):
                    t = NC * g + c
                    first = isinstance(g, int) and g == 0
                    if c == 1:
                        lo_shared(t - 1, 0)
                    h_shared(t, c % 2)
                    if c > 1 or (c == 0 and not first):
                        lo_shared(t - 1, (c + 1) % 2)
                    if c == 1 and not first:
                        sum_group(g - 1)
                    if c == (0 if first else 1):
                        split_gate_lo(g, 0)
                    if c == 2:
                        split_gate_lo(g, 2)

            def result(b, j):
                of_b = base[:, bass.ds(b, 1), :].rearrange("p a h -> p (a h)")
                dve.wait_ge(down_done, 2 * b + (NU + 2))
                dve.tensor_tensor(of_b, bank[4 + j][:, 0:H], of_b, ALU.add).then_inc(out_ready, 1)

            shared_group(0)
            with dve.Fori(1, NG) as g:
                shared_group(g)
            dve.wait_ge(setup_sb, 5)
            for n in range(4):
                h_expert(NU + n, n % 2, n // 2, n % 2)
                if n == 0:
                    lo_shared(NU - 1, 1)
                if n == 1:
                    sum_group(NG - 1)
                if n == 3:
                    dve.wait_ge(base_done, NG)
                    result(0, 0)
            with dve.Fori(1, B // 2) as i:
                n0 = dve.snap(4 * i)
                for n in range(4):
                    h_expert(n0 + (NU + n), n % 2, 2 * i + n // 2, n % 2)
                    if n == 1:
                        result(2 * i - 1, 1)
                    if n == 3:
                        result(2 * i, 0)
            result(B - 1, 1)

        @block.tensor
        def _(pe):
            pe.wait_ge(zeros_ready, 1)
            for _ in range(WARM_UP):
                pe.matmul(bank[3][:, 0:P], zeros[:, :], zeros[:, :], start=True, stop=True)
            pe.wait_ge(consts, 2)
            pe.wait_ge(cond_er_ready, 1)
            pe.transpose(bank[5][:, 0:B], cond_er[:, :, :].rearrange("b e r -> b (e r)"), ident[0:B, 0:B]
                         ).then_inc(setup_ps, 1)
            pe.wait_ge(ld_b, 16)
            pe.transpose(bank[7][:, 0:H], b_nat[:, :, :].rearrange("o e r -> o (e r)"), ident[:, :]
                         ).then_inc(setup_ps, 1)

            def x_transposes(g):
                pe.wait_ge(ld_x[g], 16)
                for j in range(GB):
                    mm = pe.transpose(bank[4 + g][:, j * S:(j + 1) * S], xn[:, g * GB + j, :], ident[:, :])
                mm.then_inc(xT_ps, 1)

            def delta_w(g):
                pe.wait_ge(sB_ready, g + 1)
                pe.matmul(bank[g][:, :], a_sb[:, :], sB[:, g % 2, :, :].rearrange("p b o -> p (b o)"),
                          start=True, stop=True).then_inc(delta_ps, 1)

            def first_layer(g):
                pe.wait_ge(weff_ready, g + 1)
                pe.wait_ge(xT_ready, g + 1)
                for j in range(GB):
                    mm = pe.matmul(bank[4 + g][:, j * S:(j + 1) * S], work[:, g, j * H:(j + 1) * H],
                                   xT[:, g * GB + j, :], start=True, stop=True)
                mm.then_inc(x1_ps, 1)

            x_transposes(0)
            pe.wait_ge(ld_w, 16)
            pe.transpose(bank[6][:, 0:H], w_nat[:, :], ident[:, :]).then_inc(setup_ps, 1)
            pe.wait_ge(ld_a, 16)
            delta_w(0)
            pe.wait_ge(setup_sb, 3)
            x_transposes(1)
            delta_w(1)
            first_layer(0)
            delta_w(2)
            x_transposes(2)
            first_layer(1)
            delta_w(3)
            x_transposes(3)
            first_layer(2)
            pe.wait_ge(rt_step, 15)
            pe.wait_ge(x1_ready, 2)
            pe.matmul(bank[5][:, 0:4 * B], ones[:, :], rdiag[:, :, :].rearrange("p k b -> p (k b)"),
                      start=True, stop=True).then_inc(setup_ps, 1)
            first_layer(3)

            def gate_up_shared(g, c):
                q = c % 2
                t = NC * g + c
                if isinstance(t, int) and t < 2:
                    pe.wait_ge(weff_ready, 2 * t + 2)
                elif isinstance(t, int) and t < 4:
                    pe.wait_ge(h_done, t - 1)
                for first, ps, done in ((G_HI, gate_ps[q], gate_done), (U_HI, up_ps[q], up_done)):
                    w_hi = wsh[:, first + c * P:first + (c + 1) * P]
                    w_lo = wsh[:, first + I + c * P:first + I + (c + 1) * P]
                    pe.matmul(ps[:, :], w_hi, x1_hi(g), start=True, stop=False)
                    pe.matmul(ps[:, :], w_hi, x1_lo(g), start=False, stop=False)
                    pe.matmul(ps[:, :], w_lo, x1_hi(g), start=False, stop=True).then_inc(done, 1)

            def down_shared(g, c):
                q = c % 2
                pe.wait_ge(lo_done, NC * g + (c + 1))
                if c == 0:
                    if isinstance(g, int) and g == 0:
                        pe.wait_ge(x1_ready, 1)
                        pe.wait_ge(sh_dlo, 1)
                    else:
                        pe.wait_ge(sum_done, g)
                w_hi = wshd[:, 0, c, :]
                w_lo = wshd[:, 1, c, :]
                pe.matmul(bank[4][:, :], w_hi, hT_hi[:, q, :], start=(c == 0), stop=False)
                pe.matmul(bank[4][:, :], w_hi, hT_lo[:, q, :], start=False, stop=False)
                pe.matmul(bank[4][:, :], w_lo, hT_hi[:, q, :], start=False, stop=(c == NC - 1)
                          ).then_inc(down_done, 1)

            def sum_transposes(g):
                pe.wait_ge(sum_done, g + 1)
                if not (isinstance(g, int) and g == 0):
                    pe.wait_ge(base_done, g)
                for j in range(GB):
                    mm = pe.transpose(bank[5][:, j * H:(j + 1) * H], s1T[:, j * S:(j + 1) * S], ident[:, :])
                mm.then_inc(sumT_done, 1)

            def expert_of(n):
                return pe.value_load(eidx[0:1, bass.ds(n, 1)], min_val=0, max_val=(E - 1) * DN)

            expert = {}

            def shared_group(g):
                first = isinstance(g, int) and g == 0
                for c in range(NC):
                    gate_up_shared(g, c)
                    if c == 1 and first:
                        pe.wait_ge(setup_sb, 5)
                        for n in range(2):
                            expert[n] = expert_of(n)
                    if c >= 2:
                        down_shared(g, c - 2)
                    elif not first:
                        down_shared(g - 1, c + 2)
                    if c == 2 and not first:
                        sum_transposes(g - 1)

            def gate_up_expert(q, j, expert, first_unit):
                w0 = pe.snap(expert * (GU // DN))
                for first, ps, done in ((G_HI, gate_ps[q], gate_done), (U_HI, up_ps[q], up_done)):
                    if first_unit and first == U_HI:
                        pe.wait_ge(ex_ulo, E)
                    w_hi = wex[:, bass.ds(w0 + first, I)]
                    w_lo = wex[:, bass.ds(w0 + (first + I), I)]
                    pe.matmul(ps[:, :], xst[:, j, 0, :], w_hi, start=True, stop=False)
                    pe.matmul(ps[:, :], xst[:, j, 1, :], w_hi, start=False, stop=False)
                    pe.matmul(ps[:, :], xst[:, j, 0, :], w_lo, start=False, stop=True).then_inc(done, 1)

            def h_transposes(n, q):
                pe.wait_ge(h_done, n + (NU + 1))
                for c in range(NC):
                    mm = pe.transpose(bank[6 + q][:, c * P:(c + 1) * P], h_sb[q][:, c * P:(c + 1) * P], ident[:, :])
                mm.then_inc(hT_done, 1)

            def down_expert(n, q, k, j, expert):
                pe.wait_ge(hT_ready, n + 1)
                for c in range(NC):
                    mm = pe.matmul(bank[4 + j][:, 0:H], hT[:, q, c * P:(c + 1) * P],
                                   wexd[:, bass.ds(expert + c * H, H)],
                                   start=(k == 0 and c == 0), stop=(k == 1 and c == NC - 1))
                mm.then_inc(down_done, 1)

            pe.wait_ge(sh_glo, 1)
            pe.wait_ge(sh_lo, 1)
            pe.wait_ge(x1lo_first, 1)
            shared_group(0)
            with pe.Fori(1, NG) as g:
                pe.wait_ge(x1lo_later, g)
                shared_group(g)
            pe.wait_ge(ex_hi, 2 * E)
            pe.wait_ge(ex_glo, E)
            for n in range(4):
                if n % 2 == 0:
                    pe.wait_ge(xst_ready, n + 2)
                gate_up_expert(n % 2, n // 2, expert[n], n == 0)
                if n == 0:
                    down_shared(NG - 1, NC - 2)
                if n < 2:
                    expert[n + 2] = expert_of(n + 2)
                if n >= 1:
                    h_transposes(n - 1, (n + 1) % 2)
                if n == 1:
                    down_shared(NG - 1, NC - 1)
                if n == 2:
                    sum_transposes(NG - 1)
                if n == 2:
                    pe.wait_ge(ld_down, 32)
                if n >= 2:
                    down_expert(n - 2, n % 2, n % 2, 0, expert[n - 2])
            pe.wait_ge(base_done, NG)
            with pe.Fori(4, NE - 3, 4) as n0:
                expert = {}
                for n in range(4):
                    expert[n] = expert_of(n0 + n)
                    if n % 2 == 0:
                        pe.wait_ge(xst_ready, n0 + (n + 2))
                    gate_up_expert(n % 2, n // 2, expert[n], False)
                    if n < 2:
                        expert[n - 2] = expert_of(n0 + (n - 2))
                    h_transposes(n0 + (n - 1), (n + 1) % 2)
                    down_expert(n0 + (n - 2), n % 2, n % 2, (n // 2 + 1) % 2, expert[n - 2])
            expert = {n: expert_of(n) for n in (NE - 2, NE - 1)}
            h_transposes(NE - 1, 1)
            down_expert(NE - 2, 0, 0, 1, expert[NE - 2])
            down_expert(NE - 1, 1, 1, 1, expert[NE - 1])


_INS = ["x", "cond_8", "L0_cond_W_base", "L0_cond_b_base", "L0_cond_As", "L0_cond_Bs",
        "L1_cond_skill_gate", "L1_cond_skill_up", "L1_cond_skill_down",
        "L1_cond_shared_gate", "L1_cond_shared_up", "L1_cond_shared_down"]
_OUTS = [((16, 128, 128), "float32")]


def kernel(**inputs):
    import numpy as _np
    import concourse.bacc as _bacc
    from concourse import mybir as _mybir
    from concourse.bass_utils import run_bass_kernel_spmd as _run

    nc = _bacc.Bacc("TRN2", target_bir_lowering=False, num_devices=1)
    arrays, args = {}, []
    for name in _INS:
        a = _np.ascontiguousarray(inputs[name])
        arrays[f"in_{name}_dram"] = a
        args.append(nc.dram_tensor(f"in_{name}_dram", a.shape, _mybir.dt.from_np(a.dtype), kind="ExternalInput").ap())
    for i, (shape, dtype) in enumerate(_OUTS):
        dt = _mybir.dt.from_np(_np.dtype(dtype))
        args.append(nc.dram_tensor(f"out_{i}_dram", shape, dt, kind="ExternalOutput").ap())
    lora_then_top2_moe(nc, *args)
    r = _run(nc, [arrays], core_ids=[0])
    return r.results[0]["out_0_dram"]
```
